# Optimizing a Trainium2 kernel written in Bass

```python
import numpy as np
import jax
import jax.numpy as jnp

def _softmax(x, axis=-1):
    return jax.nn.softmax(x, axis=axis)

def _gelu(x):
    return jax.nn.gelu(x, approximate=True)

def _silu(x):
    return jax.nn.silu(x)

def _sigmoid(x):
    return jax.nn.sigmoid(x)

def _layernorm(x, axis=-1, eps=1e-05):
    m = jnp.mean(x, axis=axis, keepdims=True)
    v = jnp.var(x, axis=axis, keepdims=True)
    return (x - m) / jnp.sqrt(v + eps)

def _scatter_add(tgt, idx, src, axis=0):
    return tgt.at[idx].add(src)

def _segment_sum(src, seg, n):
    return jax.ops.segment_sum(src, seg, n)
kernel_name = 'mk_adaln_ffn_d4_seqx_r8_4032bf'

def setup_inputs(seed: int=0):
    np.random.seed(seed)
    _w = jnp.asarray

    def _rec_inputs():
        import jax
        import jax.numpy as jnp
        _rk = jax.random.key(seed)
        x = -0.000125 + 0.9999 * jax.random.normal(jax.random.fold_in(_rk, 1), (4, 256, 256), jnp.float32)
        _lenS = 256 - jax.random.randint(jax.random.fold_in(_rk, 7), (4,), 0, max(1, 256 // 4) + 1, jnp.int32)
        _lenS2 = 256 - jax.random.randint(jax.random.fold_in(_rk, 8), (4,), 0, max(1, 256 // 4) + 1, jnp.int32)
        fside_BxSxS_0 = -1.52775e-05 + 0.999936 * jax.random.normal(jax.random.fold_in(_rk, 11), (4, 256, 256), jnp.float32)
        cond_512 = -5.03954e-05 + 1.00559 * jax.random.normal(jax.random.fold_in(_rk, 12), (4, 64), jnp.float32)
        return (x, fside_BxSxS_0, cond_512)
    x, fside_BxSxS_0, cond_512 = _rec_inputs()

    def _L0_cond_setup():
        import jax, jax.numpy as jnp
        from jax import lax
        import numpy as np
        B, T, C, TD = (8, 256, 256, 64)

        def _bi_wkv(r, k, v, w, u, time_emb):
            tf = jax.nn.sigmoid(jnp.sum(time_emb, axis=-1))[:, None, None]
            decay = jnp.exp(-jnp.exp(w.astype(jnp.float32)))[None, :] * (0.5 + 0.5 * tf[:, :, 0])
            kf = k.astype(jnp.float32)
            vf = v.astype(jnp.float32)
            ek = jnp.exp(jnp.minimum(kf, 30.0))
            ekv = ek * vf

            def step(carry, x):
                a, b = carry
                ekv_t, ek_t = x
                a = a * decay + ekv_t
                b = b * decay + ek_t
                return ((a, b), (a, b))
            ekv_t = jnp.swapaxes(ekv, 0, 1)
            ek_t = jnp.swapaxes(ek, 0, 1)
            init = (jnp.zeros_like(decay), jnp.zeros_like(decay))
            _, (nf, df) = lax.scan(step, init, (ekv_t, ek_t))
            _, (nb, db) = lax.scan(step, init, (ekv_t, ek_t), reverse=True)
            nf = jnp.swapaxes(nf, 0, 1)
            df = jnp.swapaxes(df, 0, 1)
            nb = jnp.swapaxes(nb, 0, 1)
            db = jnp.swapaxes(db, 0, 1)
            euk = jnp.exp(jnp.minimum(u.astype(jnp.float32)[None, None, :] + kf, 30.0))
            num = nf + nb - ekv + euk * vf
            den = df + db - ek + euk
            base = jax.nn.sigmoid(r.astype(jnp.float32)) * (num / jnp.maximum(den, 1e-08))
            out = base * (0.8 + 0.2 * tf)
            return out.astype(r.dtype)
        key = jax.random.key(seed)
        ks = jax.random.split(key, 6)
        return {'r': jax.random.normal(ks[0], (B, T, C), dtype=jnp.float32), 'k': jax.random.normal(ks[1], (B, T, C), dtype=jnp.float32), 'v': jax.random.normal(ks[2], (B, T, C), dtype=jnp.float32), 'w': jax.random.normal(ks[3], (C,), dtype=jnp.float32), 'u': jax.random.normal(ks[4], (C,), dtype=jnp.float32), 'time_emb': jax.random.normal(ks[5], (B, TD), dtype=jnp.float32)}
    _L0_cond_all = _L0_cond_setup()
    _L0_cond_in = {k: v for k, v in _L0_cond_all.items() if k in ('w', 'u')}
    del _L0_cond_all

    def _L0_ffn_setup():
        import jax, jax.numpy as jnp
        import numpy as np
        CAPACITY = 0.125
        HEAD_DIM = 128
        N_HEADS = 16
        N_KV_HEADS = 8
        ROPE_THETA = 10000.0
        EPS = 1e-06

        def _rms_norm(x, w):
            return x * jax.lax.rsqrt(jnp.mean(x * x, axis=-1, keepdims=True) + EPS) * w

        def _rotate_half(t):
            h = t.shape[-1] // 2
            return jnp.concatenate([-t[..., h:], t[..., :h]], axis=-1)
        key = jax.random.key(seed)
        ks = jax.random.split(key, 12)
        B, T, D = (4, 512, 256)
        I = 1024
        s = 0.02
        return {'hidden_states': jax.random.normal(ks[0], (B, T, D), jnp.float32), 'w_router': jax.random.normal(ks[1], (D,), jnp.float32) * s, 'wq': jax.random.normal(ks[2], (D, N_HEADS * HEAD_DIM), jnp.float32) * s, 'bq': jnp.zeros((N_HEADS * HEAD_DIM,), jnp.float32), 'wk': jax.random.normal(ks[3], (D, N_KV_HEADS * HEAD_DIM), jnp.float32) * s, 'bk': jnp.zeros((N_KV_HEADS * HEAD_DIM,), jnp.float32), 'wv': jax.random.normal(ks[4], (D, N_KV_HEADS * HEAD_DIM), jnp.float32) * s, 'bv': jnp.zeros((N_KV_HEADS * HEAD_DIM,), jnp.float32), 'wo': jax.random.normal(ks[5], (N_HEADS * HEAD_DIM, D), jnp.float32) * s, 'w_gate': jax.random.normal(ks[6], (D, I), jnp.float32) * s, 'w_up': jax.random.normal(ks[7], (D, I), jnp.float32) * s, 'w_down': jax.random.normal(ks[8], (I, D), jnp.float32) * s, 'ln1_w': jnp.ones((D,), jnp.float32), 'ln2_w': jnp.ones((D,), jnp.float32)}
    _L0_ffn_all = _L0_ffn_setup()
    _L0_ffn_in = {k: v for k, v in _L0_ffn_all.items() if k in ('w_router', 'wq', 'bq', 'wk', 'bk', 'wv', 'bv', 'wo', 'w_gate', 'w_up', 'w_down', 'ln1_w', 'ln2_w')}
    del _L0_ffn_all

    def _L1_cond_setup():
        import jax, jax.numpy as jnp
        from jax import lax
        import numpy as np
        B, T, C, TD = (8, 256, 256, 64)

        def _bi_wkv(r, k, v, w, u, time_emb):
            tf = jax.nn.sigmoid(jnp.sum(time_emb, axis=-1))[:, None, None]
            decay = jnp.exp(-jnp.exp(w.astype(jnp.float32)))[None, :] * (0.5 + 0.5 * tf[:, :, 0])
            kf = k.astype(jnp.float32)
            vf = v.astype(jnp.float32)
            ek = jnp.exp(jnp.minimum(kf, 30.0))
            ekv = ek * vf

            def step(carry, x):
                a, b = carry
                ekv_t, ek_t = x
                a = a * decay + ekv_t
                b = b * decay + ek_t
                return ((a, b), (a, b))
            ekv_t = jnp.swapaxes(ekv, 0, 1)
            ek_t = jnp.swapaxes(ek, 0, 1)
            init = (jnp.zeros_like(decay), jnp.zeros_like(decay))
            _, (nf, df) = lax.scan(step, init, (ekv_t, ek_t))
            _, (nb, db) = lax.scan(step, init, (ekv_t, ek_t), reverse=True)
            nf = jnp.swapaxes(nf, 0, 1)
            df = jnp.swapaxes(df, 0, 1)
            nb = jnp.swapaxes(nb, 0, 1)
            db = jnp.swapaxes(db, 0, 1)
            euk = jnp.exp(jnp.minimum(u.astype(jnp.float32)[None, None, :] + kf, 30.0))
            num = nf + nb - ekv + euk * vf
            den = df + db - ek + euk
            base = jax.nn.sigmoid(r.astype(jnp.float32)) * (num / jnp.maximum(den, 1e-08))
            out = base * (0.8 + 0.2 * tf)
            return out.astype(r.dtype)
        key = jax.random.key(seed)
        ks = jax.random.split(key, 6)
        return {'r': jax.random.normal(ks[0], (B, T, C), dtype=jnp.float32), 'k': jax.random.normal(ks[1], (B, T, C), dtype=jnp.float32), 'v': jax.random.normal(ks[2], (B, T, C), dtype=jnp.float32), 'w': jax.random.normal(ks[3], (C,), dtype=jnp.float32), 'u': jax.random.normal(ks[4], (C,), dtype=jnp.float32), 'time_emb': jax.random.normal(ks[5], (B, TD), dtype=jnp.float32)}
    _L1_cond_all = _L1_cond_setup()
    _L1_cond_in = {k: v for k, v in _L1_cond_all.items() if k in ('w', 'u')}
    del _L1_cond_all

    def _L1_ffn_setup():
        import jax, jax.numpy as jnp
        import numpy as np
        E, K, H, F = (64, 6, 256, 96)
        G, KG = (8, 4)
        SHARED_F = 96
        SCALE = 2.5
        T = 2 * 128
        CAP = 2 * (T * K // E)

        def _grouped_topk(logits, bias):
            scores = jax.nn.sigmoid(logits.astype(jnp.float32))
            scores_b = scores + bias[None, :]
            gs = scores_b.reshape(-1, G, E // G)
            group_scores = jnp.sum(jax.lax.top_k(gs, 2)[0], axis=-1)
            gidx = jax.lax.top_k(group_scores, KG)[1]
            rows = jnp.arange(group_scores.shape[0])[:, None]
            group_mask = jnp.zeros_like(group_scores).at[rows, gidx].set(1.0)
            score_mask = jnp.repeat(group_mask, E // G, axis=-1) > 0
            tmp = jnp.where(score_mask, scores_b, -jnp.inf)
            topk_ids = jax.lax.top_k(tmp, K)[1]
            topk_w = jnp.take_along_axis(scores, topk_ids, axis=-1)
            topk_w = topk_w / jnp.sum(topk_w, axis=-1, keepdims=True)
            return (topk_w * SCALE, topk_ids)

        def _routed_moe(x, topk_w, topk_ids, w_gate, w_up, w_down):
            Tn = x.shape[0]
            flat_e = topk_ids.reshape(-1)
            order = jnp.argsort(flat_e)
            se = flat_e[order]
            pos = jnp.arange(Tn * K) - jnp.searchsorted(se, se, side='left')
            tok = order // K
            valid = pos < CAP
            slot = jnp.where(valid, pos, CAP)
            buf = jnp.zeros((E, CAP + 1, H), x.dtype).at[se, slot].set(x[tok])[:, :CAP]
            h = jax.nn.silu(jnp.einsum('ech,ehf->ecf', buf, w_gate)) * jnp.einsum('ech,ehf->ecf', buf, w_up)
            out = jnp.einsum('ecf,efh->ech', h, w_down)
            gathered = out[se, jnp.minimum(pos, CAP - 1)] * valid.astype(x.dtype)[:, None]
            w = topk_w.reshape(-1)[order].astype(x.dtype)[:, None]
            return jax.ops.segment_sum(gathered * w, tok, num_segments=Tn)
        key = jax.random.key(seed)
        ks = jax.random.split(key, 9)
        s = 0.02
        return dict(hidden_states=jax.random.normal(ks[0], (2, 128, H), jnp.float32), gate_w=jax.random.normal(ks[1], (H, E), jnp.float32) * s, bias=jax.random.normal(ks[2], (E,), jnp.float32) * s, w_gate=jax.random.normal(ks[3], (E, H, F), jnp.float32) * s, w_up=jax.random.normal(ks[4], (E, H, F), jnp.float32) * s, w_down=jax.random.normal(ks[5], (E, F, H), jnp.float32) * s, ws_gate=jax.random.normal(ks[6], (H, SHARED_F), jnp.float32) * s, ws_up=jax.random.normal(ks[7], (H, SHARED_F), jnp.float32) * s, ws_down=jax.random.normal(ks[8], (SHARED_F, H), jnp.float32) * s)
    _L1_ffn_all = _L1_ffn_setup()
    _L1_ffn_in = {k: v for k, v in _L1_ffn_all.items() if k in ('gate_w', 'bias', 'w_gate', 'w_up', 'w_down', 'ws_gate', 'ws_up', 'ws_down')}
    del _L1_ffn_all

    def _L2_cond_setup():
        import jax, jax.numpy as jnp
        from jax import lax
        import numpy as np
        B, T, C, TD = (8, 256, 256, 64)

        def _bi_wkv(r, k, v, w, u, time_emb):
            tf = jax.nn.sigmoid(jnp.sum(time_emb, axis=-1))[:, None, None]
            decay = jnp.exp(-jnp.exp(w.astype(jnp.float32)))[None, :] * (0.5 + 0.5 * tf[:, :, 0])
            kf = k.astype(jnp.float32)
            vf = v.astype(jnp.float32)
            ek = jnp.exp(jnp.minimum(kf, 30.0))
            ekv = ek * vf

            def step(carry, x):
                a, b = carry
                ekv_t, ek_t = x
                a = a * decay + ekv_t
                b = b * decay + ek_t
                return ((a, b), (a, b))
            ekv_t = jnp.swapaxes(ekv, 0, 1)
            ek_t = jnp.swapaxes(ek, 0, 1)
            init = (jnp.zeros_like(decay), jnp.zeros_like(decay))
            _, (nf, df) = lax.scan(step, init, (ekv_t, ek_t))
            _, (nb, db) = lax.scan(step, init, (ekv_t, ek_t), reverse=True)
            nf = jnp.swapaxes(nf, 0, 1)
            df = jnp.swapaxes(df, 0, 1)
            nb = jnp.swapaxes(nb, 0, 1)
            db = jnp.swapaxes(db, 0, 1)
            euk = jnp.exp(jnp.minimum(u.astype(jnp.float32)[None, None, :] + kf, 30.0))
            num = nf + nb - ekv + euk * vf
            den = df + db - ek + euk
            base = jax.nn.sigmoid(r.astype(jnp.float32)) * (num / jnp.maximum(den, 1e-08))
            out = base * (0.8 + 0.2 * tf)
            return out.astype(r.dtype)
        key = jax.random.key(seed)
        ks = jax.random.split(key, 6)
        return {'r': jax.random.normal(ks[0], (B, T, C), dtype=jnp.float32), 'k': jax.random.normal(ks[1], (B, T, C), dtype=jnp.float32), 'v': jax.random.normal(ks[2], (B, T, C), dtype=jnp.float32), 'w': jax.random.normal(ks[3], (C,), dtype=jnp.float32), 'u': jax.random.normal(ks[4], (C,), dtype=jnp.float32), 'time_emb': jax.random.normal(ks[5], (B, TD), dtype=jnp.float32)}
    _L2_cond_all = _L2_cond_setup()
    _L2_cond_in = {k: v for k, v in _L2_cond_all.items() if k in ('w', 'u')}
    del _L2_cond_all

    def _L2_ffn_setup():
        import jax, jax.numpy as jnp
        import numpy as np
        NUM_EXPERTS = 8
        TOP_K = 2
        LORA_ALPHA = 2.0
        LORA_RANK = 16
        D_MODEL = 256
        D_HIDDEN = 704
        key = jax.random.key(seed)
        ks = jax.random.split(key, 11)
        B, S, D, H, E, R = (2, 128, D_MODEL, D_HIDDEN, NUM_EXPERTS, LORA_RANK)
        sd = 1.0 / np.sqrt(D)
        sh = 1.0 / np.sqrt(H)
        x = jax.random.normal(ks[0], (B, S, D), jnp.float32)
        gate_w = jax.random.normal(ks[1], (E, D), jnp.float32) * sd
        w_up = jax.random.normal(ks[2], (H, D), jnp.float32) * sd
        w_gate = jax.random.normal(ks[3], (H, D), jnp.float32) * sd
        w_down = jax.random.normal(ks[4], (D, H), jnp.float32) * sh
        up_A = jax.random.normal(ks[5], (E, R, D), jnp.float32) * sd
        up_B = jax.random.normal(ks[6], (E, H, R), jnp.float32) * 0.02
        gate_A = jax.random.normal(ks[7], (E, R, D), jnp.float32) * sd
        gate_B = jax.random.normal(ks[8], (E, H, R), jnp.float32) * 0.02
        down_A = jax.random.normal(ks[9], (E, R, H), jnp.float32) * sh
        down_B = jax.random.normal(ks[10], (E, D, R), jnp.float32) * 0.02
        return {'x': x, 'gate_w': gate_w, 'w_up': w_up, 'w_gate': w_gate, 'w_down': w_down, 'up_A': up_A, 'up_B': up_B, 'gate_A': gate_A, 'gate_B': gate_B, 'down_A': down_A, 'down_B': down_B}
    _L2_ffn_all = _L2_ffn_setup()
    _L2_ffn_in = {k: v for k, v in _L2_ffn_all.items() if k in ('gate_w', 'w_up', 'w_gate', 'w_down', 'up_A', 'up_B', 'gate_A', 'gate_B', 'down_A', 'down_B')}
    del _L2_ffn_all

    def _L3_cond_setup():
        import jax, jax.numpy as jnp
        from jax import lax
        import numpy as np
        B, T, C, TD = (8, 256, 256, 64)

        def _bi_wkv(r, k, v, w, u, time_emb):
            tf = jax.nn.sigmoid(jnp.sum(time_emb, axis=-1))[:, None, None]
            decay = jnp.exp(-jnp.exp(w.astype(jnp.float32)))[None, :] * (0.5 + 0.5 * tf[:, :, 0])
            kf = k.astype(jnp.float32)
            vf = v.astype(jnp.float32)
            ek = jnp.exp(jnp.minimum(kf, 30.0))
            ekv = ek * vf

            def step(carry, x):
                a, b = carry
                ekv_t, ek_t = x
                a = a * decay + ekv_t
                b = b * decay + ek_t
                return ((a, b), (a, b))
            ekv_t = jnp.swapaxes(ekv, 0, 1)
            ek_t = jnp.swapaxes(ek, 0, 1)
            init = (jnp.zeros_like(decay), jnp.zeros_like(decay))
            _, (nf, df) = lax.scan(step, init, (ekv_t, ek_t))
            _, (nb, db) = lax.scan(step, init, (ekv_t, ek_t), reverse=True)
            nf = jnp.swapaxes(nf, 0, 1)
            df = jnp.swapaxes(df, 0, 1)
            nb = jnp.swapaxes(nb, 0, 1)
            db = jnp.swapaxes(db, 0, 1)
            euk = jnp.exp(jnp.minimum(u.astype(jnp.float32)[None, None, :] + kf, 30.0))
            num = nf + nb - ekv + euk * vf
            den = df + db - ek + euk
            base = jax.nn.sigmoid(r.astype(jnp.float32)) * (num / jnp.maximum(den, 1e-08))
            out = base * (0.8 + 0.2 * tf)
            return out.astype(r.dtype)
        key = jax.random.key(seed)
        ks = jax.random.split(key, 6)
        return {'r': jax.random.normal(ks[0], (B, T, C), dtype=jnp.float32), 'k': jax.random.normal(ks[1], (B, T, C), dtype=jnp.float32), 'v': jax.random.normal(ks[2], (B, T, C), dtype=jnp.float32), 'w': jax.random.normal(ks[3], (C,), dtype=jnp.float32), 'u': jax.random.normal(ks[4], (C,), dtype=jnp.float32), 'time_emb': jax.random.normal(ks[5], (B, TD), dtype=jnp.float32)}
    _L3_cond_all = _L3_cond_setup()
    _L3_cond_in = {k: v for k, v in _L3_cond_all.items() if k in ('w', 'u')}
    del _L3_cond_all

    def _L3_ffn_setup():
        import jax, jax.numpy as jnp
        import numpy as np
        BF16 = jnp.bfloat16
        E4M3 = jnp.float8_e4m3fn
        FEATURES = 256
        HIDDEN = 1024
        B, S = (4, 256)

        def _qdot(x, w, out_dtype=BF16):
            return jnp.dot(x.astype(E4M3), w.astype(E4M3), preferred_element_type=out_dtype)
        key = jax.random.key(seed)
        k1, k2, k3 = jax.random.split(key, 3)
        x = jax.random.normal(k1, (B, S, FEATURES), dtype=BF16)
        w_gating = jax.random.normal(k2, (2, FEATURES, HIDDEN), dtype=jnp.float32) / np.sqrt(FEATURES)
        w_linear = jax.random.normal(k3, (HIDDEN, FEATURES), dtype=jnp.float32) / np.sqrt(HIDDEN)
        return {'x': x, 'w_gating': w_gating, 'w_linear': w_linear}
    _L3_ffn_all = _L3_ffn_setup()
    _L3_ffn_in = {k: v for k, v in _L3_ffn_all.items() if k in ('w_gating', 'w_linear')}
    del _L3_ffn_all
    return {'x': x, 'fside_BxSxS_0': fside_BxSxS_0, 'cond_512': cond_512, 'L0_cond_w': _L0_cond_in['w'], 'L0_cond_u': _L0_cond_in['u'], 'L0_ffn_w_router': _L0_ffn_in['w_router'], 'L0_ffn_wq': _L0_ffn_in['wq'], 'L0_ffn_bq': _L0_ffn_in['bq'], 'L0_ffn_wk': _L0_ffn_in['wk'], 'L0_ffn_bk': _L0_ffn_in['bk'], 'L0_ffn_wv': _L0_ffn_in['wv'], 'L0_ffn_bv': _L0_ffn_in['bv'], 'L0_ffn_wo': _L0_ffn_in['wo'], 'L0_ffn_w_gate': _L0_ffn_in['w_gate'], 'L0_ffn_w_up': _L0_ffn_in['w_up'], 'L0_ffn_w_down': _L0_ffn_in['w_down'], 'L0_ffn_ln1_w': _L0_ffn_in['ln1_w'], 'L0_ffn_ln2_w': _L0_ffn_in['ln2_w'], 'L1_cond_w': _L1_cond_in['w'], 'L1_cond_u': _L1_cond_in['u'], 'L1_ffn_gate_w': _L1_ffn_in['gate_w'], 'L1_ffn_bias': _L1_ffn_in['bias'], 'L1_ffn_w_gate': _L1_ffn_in['w_gate'], 'L1_ffn_w_up': _L1_ffn_in['w_up'], 'L1_ffn_w_down': _L1_ffn_in['w_down'], 'L1_ffn_ws_gate': _L1_ffn_in['ws_gate'], 'L1_ffn_ws_up': _L1_ffn_in['ws_up'], 'L1_ffn_ws_down': _L1_ffn_in['ws_down'], 'L2_cond_w': _L2_cond_in['w'], 'L2_cond_u': _L2_cond_in['u'], 'L2_ffn_gate_w': _L2_ffn_in['gate_w'], 'L2_ffn_w_up': _L2_ffn_in['w_up'], 'L2_ffn_w_gate': _L2_ffn_in['w_gate'], 'L2_ffn_w_down': _L2_ffn_in['w_down'], 'L2_ffn_up_A': _L2_ffn_in['up_A'], 'L2_ffn_up_B': _L2_ffn_in['up_B'], 'L2_ffn_gate_A': _L2_ffn_in['gate_A'], 'L2_ffn_gate_B': _L2_ffn_in['gate_B'], 'L2_ffn_down_A': _L2_ffn_in['down_A'], 'L2_ffn_down_B': _L2_ffn_in['down_B'], 'L3_cond_w': _L3_cond_in['w'], 'L3_cond_u': _L3_cond_in['u'], 'L3_ffn_w_gating': _L3_ffn_in['w_gating'], 'L3_ffn_w_linear': _L3_ffn_in['w_linear']}

def reference(x, fside_BxSxS_0, cond_512, L0_cond_w, L0_cond_u, L0_ffn_w_router, L0_ffn_wq, L0_ffn_bq, L0_ffn_wk, L0_ffn_bk, L0_ffn_wv, L0_ffn_bv, L0_ffn_wo, L0_ffn_w_gate, L0_ffn_w_up, L0_ffn_w_down, L0_ffn_ln1_w, L0_ffn_ln2_w, L1_cond_w, L1_cond_u, L1_ffn_gate_w, L1_ffn_bias, L1_ffn_w_gate, L1_ffn_w_up, L1_ffn_w_down, L1_ffn_ws_gate, L1_ffn_ws_up, L1_ffn_ws_down, L2_cond_w, L2_cond_u, L2_ffn_gate_w, L2_ffn_w_up, L2_ffn_w_gate, L2_ffn_w_down, L2_ffn_up_A, L2_ffn_up_B, L2_ffn_gate_A, L2_ffn_gate_B, L2_ffn_down_A, L2_ffn_down_B, L3_cond_w, L3_cond_u, L3_ffn_w_gating, L3_ffn_w_linear):
    import jax
    import jax.numpy as jnp

    def _L0_cond_ref(r, k, v, w, u, time_emb):
        import jax, jax.numpy as jnp
        from jax import lax
        import numpy as np
        B, T, C, TD = (8, 256, 256, 64)

        def _bi_wkv(r, k, v, w, u, time_emb):
            tf = jax.nn.sigmoid(jnp.sum(time_emb, axis=-1))[:, None, None]
            decay = jnp.exp(-jnp.exp(w.astype(jnp.float32)))[None, :] * (0.5 + 0.5 * tf[:, :, 0])
            kf = k.astype(jnp.float32)
            vf = v.astype(jnp.float32)
            ek = jnp.exp(jnp.minimum(kf, 30.0))
            ekv = ek * vf

            def step(carry, x):
                a, b = carry
                ekv_t, ek_t = x
                a = a * decay + ekv_t
                b = b * decay + ek_t
                return ((a, b), (a, b))
            ekv_t = jnp.swapaxes(ekv, 0, 1)
            ek_t = jnp.swapaxes(ek, 0, 1)
            init = (jnp.zeros_like(decay), jnp.zeros_like(decay))
            _, (nf, df) = lax.scan(step, init, (ekv_t, ek_t))
            _, (nb, db) = lax.scan(step, init, (ekv_t, ek_t), reverse=True)
            nf = jnp.swapaxes(nf, 0, 1)
            df = jnp.swapaxes(df, 0, 1)
            nb = jnp.swapaxes(nb, 0, 1)
            db = jnp.swapaxes(db, 0, 1)
            euk = jnp.exp(jnp.minimum(u.astype(jnp.float32)[None, None, :] + kf, 30.0))
            num = nf + nb - ekv + euk * vf
            den = df + db - ek + euk
            base = jax.nn.sigmoid(r.astype(jnp.float32)) * (num / jnp.maximum(den, 1e-08))
            out = base * (0.8 + 0.2 * tf)
            return out.astype(r.dtype)
        return _bi_wkv(r, k, v, w, u, time_emb)

    def _L0_ffn_ref(hidden_states, w_router, wq, bq, wk, bk, wv, bv, wo, w_gate, w_up, w_down, ln1_w, ln2_w):
        import jax, jax.numpy as jnp
        import numpy as np
        CAPACITY = 0.125
        HEAD_DIM = 128
        N_HEADS = 16
        N_KV_HEADS = 8
        ROPE_THETA = 10000.0
        EPS = 1e-06

        def _rms_norm(x, w):
            return x * jax.lax.rsqrt(jnp.mean(x * x, axis=-1, keepdims=True) + EPS) * w

        def _rotate_half(t):
            h = t.shape[-1] // 2
            return jnp.concatenate([-t[..., h:], t[..., :h]], axis=-1)
        B, T, D = hidden_states.shape
        k = max(1, int(T * CAPACITY))
        scores = jnp.einsum('btd,d->bt', hidden_states, w_router)
        _, idx = jax.lax.top_k(scores, k)
        idx = jnp.sort(idx, axis=-1)
        b = jnp.arange(B)[:, None]
        sel = hidden_states[b, idx]
        sel_scores = scores[b, idx]
        S = B * k
        x = sel.reshape(S, D)
        pos = idx.reshape(S)
        inv_freq = 1.0 / ROPE_THETA ** (jnp.arange(0, HEAD_DIM, 2, dtype=jnp.float32) / HEAD_DIM)
        ang = pos.astype(jnp.float32)[:, None] * inv_freq
        cos = jnp.concatenate([jnp.cos(ang), jnp.cos(ang)], axis=-1)[:, None, :]
        sin = jnp.concatenate([jnp.sin(ang), jnp.sin(ang)], axis=-1)[:, None, :]
        h = _rms_norm(x, ln1_w)
        q = (h @ wq + bq).reshape(S, N_HEADS, HEAD_DIM)
        kk = (h @ wk + bk).reshape(S, N_KV_HEADS, HEAD_DIM)
        v = (h @ wv + bv).reshape(S, N_KV_HEADS, HEAD_DIM)
        q = q * cos + _rotate_half(q) * sin
        kk = kk * cos + _rotate_half(kk) * sin
        rep = N_HEADS // N_KV_HEADS
        kk = jnp.repeat(kk, rep, axis=1)
        v = jnp.repeat(v, rep, axis=1)
        att = jnp.einsum('shd,thd->hst', q, kk) / np.sqrt(HEAD_DIM)
        causal = jnp.tril(jnp.ones((S, S), bool))
        att = jnp.where(causal[None], att, jnp.finfo(att.dtype).min)
        att = jax.nn.softmax(att, axis=-1)
        attn_out = jnp.einsum('hst,thd->shd', att, v).reshape(S, N_HEADS * HEAD_DIM) @ wo
        x1 = x + attn_out
        h2 = _rms_norm(x1, ln2_w)
        mlp = jax.nn.silu(h2 @ w_gate) * (h2 @ w_up) @ w_down
        processed = x1 + mlp
        gate = jax.nn.sigmoid(sel_scores).reshape(S, 1)
        gated = gate * processed + (1.0 - gate) * x
        output = hidden_states.at[b, idx].set(gated.reshape(B, k, D))
        return output

    def _L1_cond_ref(r, k, v, w, u, time_emb):
        import jax, jax.numpy as jnp
        from jax import lax
        import numpy as np
        B, T, C, TD = (8, 256, 256, 64)

        def _bi_wkv(r, k, v, w, u, time_emb):
            tf = jax.nn.sigmoid(jnp.sum(time_emb, axis=-1))[:, None, None]
            decay = jnp.exp(-jnp.exp(w.astype(jnp.float32)))[None, :] * (0.5 + 0.5 * tf[:, :, 0])
            kf = k.astype(jnp.float32)
            vf = v.astype(jnp.float32)
            ek = jnp.exp(jnp.minimum(kf, 30.0))
            ekv = ek * vf

            def step(carry, x):
                a, b = carry
                ekv_t, ek_t = x
                a = a * decay + ekv_t
                b = b * decay + ek_t
                return ((a, b), (a, b))
            ekv_t = jnp.swapaxes(ekv, 0, 1)
            ek_t = jnp.swapaxes(ek, 0, 1)
            init = (jnp.zeros_like(decay), jnp.zeros_like(decay))
            _, (nf, df) = lax.scan(step, init, (ekv_t, ek_t))
            _, (nb, db) = lax.scan(step, init, (ekv_t, ek_t), reverse=True)
            nf = jnp.swapaxes(nf, 0, 1)
            df = jnp.swapaxes(df, 0, 1)
            nb = jnp.swapaxes(nb, 0, 1)
            db = jnp.swapaxes(db, 0, 1)
            euk = jnp.exp(jnp.minimum(u.astype(jnp.float32)[None, None, :] + kf, 30.0))
            num = nf + nb - ekv + euk * vf
            den = df + db - ek + euk
            base = jax.nn.sigmoid(r.astype(jnp.float32)) * (num / jnp.maximum(den, 1e-08))
            out = base * (0.8 + 0.2 * tf)
            return out.astype(r.dtype)
        return _bi_wkv(r, k, v, w, u, time_emb)

    def _L1_ffn_ref(hidden_states, gate_w, bias, w_gate, w_up, w_down, ws_gate, ws_up, ws_down):
        import jax, jax.numpy as jnp
        import numpy as np
        E, K, H, F = (64, 6, 256, 96)
        G, KG = (8, 4)
        SHARED_F = 96
        SCALE = 2.5
        T = 2 * 128
        CAP = 2 * (T * K // E)

        def _grouped_topk(logits, bias):
            scores = jax.nn.sigmoid(logits.astype(jnp.float32))
            scores_b = scores + bias[None, :]
            gs = scores_b.reshape(-1, G, E // G)
            group_scores = jnp.sum(jax.lax.top_k(gs, 2)[0], axis=-1)
            gidx = jax.lax.top_k(group_scores, KG)[1]
            rows = jnp.arange(group_scores.shape[0])[:, None]
            group_mask = jnp.zeros_like(group_scores).at[rows, gidx].set(1.0)
            score_mask = jnp.repeat(group_mask, E // G, axis=-1) > 0
            tmp = jnp.where(score_mask, scores_b, -jnp.inf)
            topk_ids = jax.lax.top_k(tmp, K)[1]
            topk_w = jnp.take_along_axis(scores, topk_ids, axis=-1)
            topk_w = topk_w / jnp.sum(topk_w, axis=-1, keepdims=True)
            return (topk_w * SCALE, topk_ids)

        def _routed_moe(x, topk_w, topk_ids, w_gate, w_up, w_down):
            Tn = x.shape[0]
            flat_e = topk_ids.reshape(-1)
            order = jnp.argsort(flat_e)
            se = flat_e[order]
            pos = jnp.arange(Tn * K) - jnp.searchsorted(se, se, side='left')
            tok = order // K
            valid = pos < CAP
            slot = jnp.where(valid, pos, CAP)
            buf = jnp.zeros((E, CAP + 1, H), x.dtype).at[se, slot].set(x[tok])[:, :CAP]
            h = jax.nn.silu(jnp.einsum('ech,ehf->ecf', buf, w_gate)) * jnp.einsum('ech,ehf->ecf', buf, w_up)
            out = jnp.einsum('ecf,efh->ech', h, w_down)
            gathered = out[se, jnp.minimum(pos, CAP - 1)] * valid.astype(x.dtype)[:, None]
            w = topk_w.reshape(-1)[order].astype(x.dtype)[:, None]
            return jax.ops.segment_sum(gathered * w, tok, num_segments=Tn)
        orig_shape = hidden_states.shape
        x = hidden_states.reshape(-1, H)
        router_logits = x @ gate_w
        topk_w, topk_ids = _grouped_topk(router_logits, bias)
        y = _routed_moe(x, topk_w, topk_ids, w_gate, w_up, w_down)
        shared = jax.nn.silu(x @ ws_gate) * (x @ ws_up) @ ws_down
        return (y + shared).reshape(orig_shape)

    def _L2_cond_ref(r, k, v, w, u, time_emb):
        import jax, jax.numpy as jnp
        from jax import lax
        import numpy as np
        B, T, C, TD = (8, 256, 256, 64)

        def _bi_wkv(r, k, v, w, u, time_emb):
            tf = jax.nn.sigmoid(jnp.sum(time_emb, axis=-1))[:, None, None]
            decay = jnp.exp(-jnp.exp(w.astype(jnp.float32)))[None, :] * (0.5 + 0.5 * tf[:, :, 0])
            kf = k.astype(jnp.float32)
            vf = v.astype(jnp.float32)
            ek = jnp.exp(jnp.minimum(kf, 30.0))
            ekv = ek * vf

            def step(carry, x):
                a, b = carry
                ekv_t, ek_t = x
                a = a * decay + ekv_t
                b = b * decay + ek_t
                return ((a, b), (a, b))
            ekv_t = jnp.swapaxes(ekv, 0, 1)
            ek_t = jnp.swapaxes(ek, 0, 1)
            init = (jnp.zeros_like(decay), jnp.zeros_like(decay))
            _, (nf, df) = lax.scan(step, init, (ekv_t, ek_t))
            _, (nb, db) = lax.scan(step, init, (ekv_t, ek_t), reverse=True)
            nf = jnp.swapaxes(nf, 0, 1)
            df = jnp.swapaxes(df, 0, 1)
            nb = jnp.swapaxes(nb, 0, 1)
            db = jnp.swapaxes(db, 0, 1)
            euk = jnp.exp(jnp.minimum(u.astype(jnp.float32)[None, None, :] + kf, 30.0))
            num = nf + nb - ekv + euk * vf
            den = df + db - ek + euk
            base = jax.nn.sigmoid(r.astype(jnp.float32)) * (num / jnp.maximum(den, 1e-08))
            out = base * (0.8 + 0.2 * tf)
            return out.astype(r.dtype)
        return _bi_wkv(r, k, v, w, u, time_emb)

    def _L2_ffn_ref(x, gate_w, w_up, w_gate, w_down, up_A, up_B, gate_A, gate_B, down_A, down_B):
        import jax, jax.numpy as jnp
        import numpy as np
        NUM_EXPERTS = 8
        TOP_K = 2
        LORA_ALPHA = 2.0
        LORA_RANK = 16
        D_MODEL = 256
        D_HIDDEN = 704
        B, S, D = x.shape
        H = w_up.shape[0]
        gate_logits = jnp.einsum('bsd,ed->bse', x, gate_w)
        topw, sel = jax.lax.top_k(gate_logits, TOP_K)
        topw = jax.nn.softmax(topw.astype(jnp.float32), axis=1).astype(x.dtype)
        xt = x.reshape(-1, D)
        wf = topw.reshape(-1, TOP_K)
        sf = sel.reshape(-1, TOP_K)
        base_up = xt @ w_up.T
        base_gate = xt @ w_gate.T
        mixed_h = jnp.zeros((xt.shape[0], H), x.dtype)
        lora_down = jnp.zeros_like(xt)
        for e in range(NUM_EXPERTS):
            c = jnp.sum(jnp.where(sf == e, wf, 0.0), axis=1)
            lo_up = LORA_ALPHA * (xt @ up_A[e].T @ up_B[e].T)
            lo_gate = LORA_ALPHA * (xt @ gate_A[e].T @ gate_B[e].T)
            h_e = jax.nn.silu(base_up + lo_up) * (base_gate + lo_gate)
            ch = c[:, None] * h_e
            mixed_h = mixed_h + ch
            lora_down = lora_down + LORA_ALPHA * (ch @ down_A[e].T @ down_B[e].T)
        out = mixed_h @ w_down.T + lora_down
        return out.reshape(B, S, D)

    def _L3_cond_ref(r, k, v, w, u, time_emb):
        import jax, jax.numpy as jnp
        from jax import lax
        import numpy as np
        B, T, C, TD = (8, 256, 256, 64)

        def _bi_wkv(r, k, v, w, u, time_emb):
            tf = jax.nn.sigmoid(jnp.sum(time_emb, axis=-1))[:, None, None]
            decay = jnp.exp(-jnp.exp(w.astype(jnp.float32)))[None, :] * (0.5 + 0.5 * tf[:, :, 0])
            kf = k.astype(jnp.float32)
            vf = v.astype(jnp.float32)
            ek = jnp.exp(jnp.minimum(kf, 30.0))
            ekv = ek * vf

            def step(carry, x):
                a, b = carry
                ekv_t, ek_t = x
                a = a * decay + ekv_t
                b = b * decay + ek_t
                return ((a, b), (a, b))
            ekv_t = jnp.swapaxes(ekv, 0, 1)
            ek_t = jnp.swapaxes(ek, 0, 1)
            init = (jnp.zeros_like(decay), jnp.zeros_like(decay))
            _, (nf, df) = lax.scan(step, init, (ekv_t, ek_t))
            _, (nb, db) = lax.scan(step, init, (ekv_t, ek_t), reverse=True)
            nf = jnp.swapaxes(nf, 0, 1)
            df = jnp.swapaxes(df, 0, 1)
            nb = jnp.swapaxes(nb, 0, 1)
            db = jnp.swapaxes(db, 0, 1)
            euk = jnp.exp(jnp.minimum(u.astype(jnp.float32)[None, None, :] + kf, 30.0))
            num = nf + nb - ekv + euk * vf
            den = df + db - ek + euk
            base = jax.nn.sigmoid(r.astype(jnp.float32)) * (num / jnp.maximum(den, 1e-08))
            out = base * (0.8 + 0.2 * tf)
            return out.astype(r.dtype)
        return _bi_wkv(r, k, v, w, u, time_emb)

    def _L3_ffn_ref(x, w_gating, w_linear):
        import jax, jax.numpy as jnp
        import numpy as np
        BF16 = jnp.bfloat16
        E4M3 = jnp.float8_e4m3fn
        FEATURES = 256
        HIDDEN = 1024
        B, S = (4, 256)

        def _qdot(x, w, out_dtype=BF16):
            return jnp.dot(x.astype(E4M3), w.astype(E4M3), preferred_element_type=out_dtype)
        ff_gate = _qdot(x, w_gating[0])
        gate_value = jax.nn.gelu(ff_gate)
        ff1 = _qdot(x, w_gating[1])
        activations = gate_value * ff1
        outputs = _qdot(activations, w_linear)
        return outputs
    x = x + _L0_ffn_ref(_L0_cond_ref(x, fside_BxSxS_0, fside_BxSxS_0, L0_cond_w, L0_cond_u, cond_512), L0_ffn_w_router, L0_ffn_wq, L0_ffn_bq, L0_ffn_wk, L0_ffn_bk, L0_ffn_wv, L0_ffn_bv, L0_ffn_wo, L0_ffn_w_gate, L0_ffn_w_up, L0_ffn_w_down, L0_ffn_ln1_w, L0_ffn_ln2_w)
    x = x + _L1_ffn_ref(_L1_cond_ref(x, fside_BxSxS_0, fside_BxSxS_0, L1_cond_w, L1_cond_u, cond_512), L1_ffn_gate_w, L1_ffn_bias, L1_ffn_w_gate, L1_ffn_w_up, L1_ffn_w_down, L1_ffn_ws_gate, L1_ffn_ws_up, L1_ffn_ws_down)
    x = x + _L2_ffn_ref(_L2_cond_ref(x, fside_BxSxS_0, fside_BxSxS_0, L2_cond_w, L2_cond_u, cond_512), L2_ffn_gate_w, L2_ffn_w_up, L2_ffn_w_gate, L2_ffn_w_down, L2_ffn_up_A, L2_ffn_up_B, L2_ffn_gate_A, L2_ffn_gate_B, L2_ffn_down_A, L2_ffn_down_B)
    x = x + _L3_ffn_ref(_L3_cond_ref(x, fside_BxSxS_0, fside_BxSxS_0, L3_cond_w, L3_cond_u, cond_512), L3_ffn_w_gating, L3_ffn_w_linear)
    return x

_drawn_inputs = setup_inputs


def setup_inputs(seed=0):
    import zlib

    import numpy as np

    out = dict(_drawn_inputs(seed))
    spreads = {'L0_ffn_bq': (0.0, 0.8),
     'L0_ffn_bk': (0.0, 0.8),
     'L0_ffn_bv': (0.0, 0.564),
     'L0_ffn_ln1_w': (1.0, 0.6),
     'L0_ffn_ln2_w': (1.0, 0.6)}
    factors = {'L0_ffn_wq': 8.0,
     'L0_ffn_wk': 8.0,
     'L0_ffn_w_gate': 8.0,
     'L0_ffn_w_up': 8.0,
     'L0_ffn_w_down': 8.0,
     'L1_cond_w': 8.0,
     'L1_cond_u': 8.0,
     'L1_ffn_gate_w': 8.0,
     'L1_ffn_bias': 8.0,
     'L1_ffn_w_gate': 8.0,
     'L1_ffn_w_up': 8.0,
     'L1_ffn_w_down': 8.0,
     'L1_ffn_ws_gate': 8.0,
     'L1_ffn_ws_up': 8.0,
     'L1_ffn_ws_down': 8.0,
     'L2_cond_w': 8.0,
     'L2_cond_u': 8.0,
     'L2_ffn_gate_w': 8.0,
     'L2_ffn_w_up': 8.0,
     'L2_ffn_w_gate': 8.0,
     'L2_ffn_w_down': 8.0,
     'L2_ffn_up_A': 8.0,
     'L2_ffn_up_B': 8.0,
     'L2_ffn_gate_A': 8.0,
     'L2_ffn_gate_B': 8.0,
     'L2_ffn_down_A': 8.0,
     'L2_ffn_down_B': 8.0,
     'L3_cond_w': 8.0,
     'L3_cond_u': 8.0,
     'L3_ffn_w_gating': 8.0,
     'L3_ffn_w_linear': 8.0}
    for name, (base, spread) in spreads.items():
        noise = np.random.default_rng([zlib.crc32(name.encode()), seed]).standard_normal(out[name].shape)
        drawn = base * np.exp(spread * noise) if base else spread * noise
        out[name] = jnp.asarray(drawn.astype(out[name].dtype))
    for name, factor in factors.items():
        out[name] = (out[name] * factor).astype(out[name].dtype)
    return out
```

```python
from contextlib import ExitStack

import numpy as np

import concourse.bass as bass
import concourse.mybir as mybir

F32, BF16, U32, I32, I16 = (mybir.dt.float32, mybir.dt.bfloat16, mybir.dt.uint32, mybir.dt.int32, mybir.dt.int16)
ALU = mybir.AluOpType
ACT = mybir.ActivationFunctionType
AX = mybir.AxisListType

P = 128
B, T, C = 4, 256, 256
N = B * T
CT = C // P
NT = N // P
TD = 64
LAYERS = 4
CHUNK = 512
NCH = N // CHUNK

TOP = T // 8
HD, NH, NKV = 128, 16, 8
QK = NH + NKV
F0 = 1024
F0T = F0 // P
PICKED = -3e38
NOWHERE = 3e38

E1, K1, F1, G1, KG1 = 64, 6, 96, 8, 4
CAP = 2 * (2 * 128 * K1 // E1)
SLOTS = E1 * CAP
ST = SLOTS // P
GE = 8
NG = E1 // GE
GS = GE * CAP
GT = GS // P
ROW = C + E1
XRING = 12
LOW = -1e30

E2, R2, H2 = 8, 16, 704
H2T = (H2 + P - 1) // P
H2W = [min(P, H2 - i * P) for i in range(H2T)]

F3 = 1024
F3T = F3 // P
E4_MIN = 2.0 ** -6
E4_NAN = 2.0 ** 119.15

K_ID, K_IOTA, K_DESC = 0, P, P + N
K_CAUS = K_DESC + N
K_TAB = K_CAUS + P
TABW = 192
K_JM = K_TAB + 2 * TABW
K_BB = K_JM + TOP
K_EM = K_BB + 1
K_W = K_EM + ST * E1

V_W, V_U, V_WR, V_LN1, V_LN2 = 0, 8, 16, 18, 20
V_N = 22


def build(nc, I, out):
    ctx = ExitStack()
    with ctx:
        def sb(name, shape, dt=F32):
            return ctx.enter_context(nc.sbuf_tensor(name, shape, dt))

        sems = {}

        def S(name):
            if name not in sems:
                sems[name] = ctx.enter_context(nc.semaphore(name))
            return sems[name]

        xT, kT, ekT, ekvT, cT = (sb(n, [P, CT, N]) for n in ("xT", "kT", "ekT", "ekvT", "cT"))
        ratio = [sb(f"ratio{i}", [P, CT, N]) for i in range(2)]
        wA, wB, wC, wD = (sb(n, [P, CT, N]) for n in ("wkv_a", "wkv_b", "wkv_c", "wkv_d"))
        const = sb("const", [P, K_W])
        condb = sb("condb", [P, B, TD])
        wrb = sb("wrb", [P, C])
        vecs = sb("vecs", [P, V_N])
        tsum, tf, dsc, nosc = (sb(n, [P, B]) for n in ("tsum", "tf", "dsc", "nosc"))
        dw = sb("dw", [P, 2 * LAYERS])
        dec = sb("dec", [P, 2 * LAYERS, B])
        AC = 25780
        arena = sb("arena", [P, AC])
        bank = [ctx.enter_context(nc.psum_tensor(f"bank{i}", [P, CHUNK], F32)) for i in range(8)]

        scratch = nc.dram_tensor("token_rows", [N + 1, ROW], F32, kind="Internal").ap()
        slotd = nc.dram_tensor("slot_tokens", [E1, CAP], F32, kind="Internal").ap()

        ident = const[:, K_ID:K_ID + P]
        iota = const[:, K_IOTA:K_IOTA + N]
        desc = const[:, K_DESC:K_DESC + N]
        causal = const[:, K_CAUS:K_CAUS + P]
        table = const[:, K_TAB:K_TAB + 2 * TABW].rearrange("p (h c) -> p h c", h=2)
        jmask = const[:, K_JM:K_JM + TOP]
        bbase = const[:, K_BB:K_BB + 1]
        emask = const[:, K_EM:K_EM + ST * E1].rearrange("p (t e) -> p t e", e=E1)

        def at(off, *dims, rows=P):
            n = int(np.prod(dims))
            assert off + n <= AC, (off, dims)
            v = arena[0:rows, off:off + n]
            if len(dims) == 2:
                v = v.rearrange("p (a b) -> p a b", b=dims[1])
            if len(dims) == 3:
                v = v.rearrange("p (a b c) -> p a b c", b=dims[1], c=dims[2])
            return v

        wq, wk, wv = at(0, CT, NH * HD), at(4096, CT, NKV * HD), at(6144, CT, NKV * HD)
        wo = at(0, NH, C)
        wg0, wu0 = at(4096, CT, F0), at(6144, CT, F0)
        wd0 = at(8192, F0T, C)
        o = 10240
        onehot = at(o, N); o += N
        ctok0 = at(o, NT, C); onehotT = at(o + 2048, NT, P); probT = at(o, NH, P); o += 3072
        qk = at(o, QK, HD); att = at(o, NH, P)
        su0 = at(o, F0T, P); hm0 = at(o + 1024, F0T, P); o += 3072
        rot_a, rot_b = at(o, CHUNK), at(o + 512, CHUNK); o += 1024
        spread4 = at(o - 1024, P, rows=B)
        vtok = at(o, NKV, HD); o += 1024
        qkT = at(o, QK, P); oT0 = at(o, NH, P); o += 3072
        bias8 = at(o, 512, rows=8); o += 512
        xs, xn, ao, x1, dl, sq = (at(o + i * C, C) for i in range(6)); o += 6 * C
        hT0 = h2T0 = at(o, CT, P); o += CT * P
        cs = at(o, TABW); o += TABW
        wbat = at(o, CT, B * B); o += CT * B * B
        scr = at(o, T, rows=B); top4 = at(o + 256, TOP, rows=B); m8a = at(o + 288, 8, rows=B)
        vsel = at(o + 296, TOP); o += 352
        col0 = at(o, 16); o += 16
        mx0, sm0 = at(o, NH), at(o + NH, NH); o += 2 * NH
        assert o <= AC

        GW = GE * (2 * CT * F1 + C)
        ring = [dict(g=at(i * GW, GE, CT * F1), u=at(i * GW + GE * CT * F1, GE, CT * F1),
                     d=at(i * GW + 2 * GE * CT * F1, GE, C, rows=F1)) for i in range(2)]
        o = 2 * GW
        xg = at(o, XRING, ROW)
        sc1, sb1, tm1, mk1, w1 = (at(o + i * 512, NT, E1) for i in range(5))
        hi4, lo4 = at(o + 2560, 64, 4), at(o + 2816, 64, 4)
        hi2, mi2, lo2 = (at(o + 3072 + 128 * i, 64, 2) for i in range(3)); o += XRING * ROW
        xgT = [at(o + 768 * i, CT, GS) for i in range(2)]; ctok1 = at(o, NT, C); o += 1536
        outT1 = at(o, CT, GS); o += 768
        st1 = [at(o + GT * N // 2 * i, GT * N // 2).bitcast(BF16).rearrange("p (t n) -> p t n", n=N) for i in range(2)]
        o += GT * N
        PW = 3 * GT * C // 2
        part1 = [at(o, PW).bitcast(BF16).rearrange("p (s t c) -> p s t c", s=3, t=GT)]; val1 = at(o, N, rows=E1); o += 1536
        sg1, h1 = at(o, GS, rows=F1), at(o + GS, GS, rows=F1); zrow = at(o, ROW, rows=1); o += 2 * GS
        shg, shh = at(o, N, rows=F1), at(o + N, N, rows=F1); wsel = at(o, ST // 2, E1)
        part1.append(at(o + ST // 2 * E1, PW).bitcast(BF16).rearrange("p (s t c) -> p s t c", s=3, t=GT)); o += 2 * N
        gw1 = at(o, CT, E1); o += CT * E1
        wsg, wsu = at(o, CT, F1), at(o + CT * F1, CT, F1); o += 2 * CT * F1
        wsd = at(o, C, rows=F1); o += C
        bias1 = at(o, E1); o += E1
        outw = at(o, GT, C)
        gs1, m8b = at(o, NT, G1), at(o + 64, NT, 8); o += 256
        gmk, gpn = at(o + 256, 64), at(o + 320, 64); o += 384
        m8c = at(o, NT, 8); o += 192
        ws1, wr1 = at(o, NT), at(o + 8, NT); o += 16
        v48 = at(o, CAP, rows=E1); o += CAP
        slotrow = at(o, P, rows=ST); o += P
        tokf, toki, wslot = at(o, ST), at(o + ST, ST), at(o + 2 * ST, ST); o += 3 * ST
        
        m8d = at(o, 8, rows=E1); o += 8
        assert o <= AC, o

        wup2, wga2 = at(0, CT, H2), at(1408, CT, H2)
        aup, aga = at(2816, CT, P), at(3072, CT, P)
        bup, bga = at(3328, H2), at(4032, H2)
        wdn2, adn, bdn = at(5120, H2T, C), at(6656, H2T, P), at(7424, C)
        wg3 = at(7680, CT * F3).bitcast(BF16).rearrange("p (a b) -> p a b", a=CT)
        o = 10240
        zu, zg = at(o, N), at(o + N, N); lbuf = [at(o + 512 * i, 512) for i in range(8)]; o += 4096
        mt2, cw2 = at(o - 2048, N, rows=2 + 2 * E2), at(o - 1024, N, rows=2)
        spread2 = at(o + 2 * N, 2, P, rows=2 + 2 * E2)
        m1b, m2b, c1b, c2b = (at(o + N * i, N) for i in range(4)); o += 4 * N
        zu1, zud, zg1, zgd = (at(o + N * i, N) for i in range(4)); o += 4 * N
        lg2, v82, i82, i82f = (at(o + 64 * i, NT, E2) for i in range(4)); o += 256
        oh2 = at(o, NT, 2 + 2 * E2); o += NT * (2 + 2 * E2)
        s2 = at(o, 16, rows=2); gw2 = at(o + 16, CT, E2); o += 32
        wl3 = at(o, F3T * C // 2).bitcast(BF16).rearrange("p (a b) -> p a b", b=C); o += F3T * C // 2
        assert o <= AC, o

        c8 = wA[:, 0, :].bitcast(BF16).rearrange("p (a b) -> p a b", a=CT)
        mg3, tmp3 = wB, wD
        o = 10240
        g3 = [at(o + 256 * i, 256).bitcast(BF16) for i in range(2)]; o += 512
        gg3 = [at(o + 256 * i, 256).bitcast(BF16) for i in range(2)]; o += 512
        u3 = [at(o + 256 * i, 256).bitcast(BF16) for i in range(2)]; o += 512
        a3 = [at(o + 4096 + 256 * i, 256).bitcast(BF16) for i in range(2)]; e3 = at(o + 256, 256).bitcast(BF16); b3 = at(o + 512, 256).bitcast(BF16)
        n3 = at(o + 768, 256).bitcast(BF16); o += 1024
        q3 = [at(o + 256 * i, 256).bitcast(BF16) for i in range(3)]; o += 768
        y3 = [at(o + 256 * i, 256).bitcast(BF16) for i in range(2)]; o += 512
        r3 = [at(o + 512 * i, 512) for i in range(2)]; o += 1024

        block = ctx.enter_context(nc.Block())

        def l2bufs(it):
            return lbuf[0], lbuf[1], lbuf[3 + (it % 2)], lbuf[2], lbuf[5 + (it % 2)], lbuf[7]


        @block.sync
        def _(sp):
            sp.dma_start(kT[:], I["kT"]).then_inc(S("k_in"), 16)
            sp.dma_start(vecs[:], I["vecs"]).then_inc(S("vecs_in"), 16)
            sp.dma_start(condb[:], I["cond"].rearrange("(o b) t -> o b t", o=1).to_broadcast([P, B, TD])).then_inc(S("cond_in"), 16)
            sp.dma_start(xT[:], I["xT"]).then_inc(S("x_in"), 16)
            sp.dma_start(const[:], I["const"]).then_inc(S("const_in"), 16)
            sp.dma_start(wrb[:], I["w_router"].rearrange("(o c) -> o c", o=1).to_broadcast([P, C])).then_inc(S("wrb_in"), 16)
            sp.dma_start(bias8, I["qkv_b"]).then_inc(S("bias8_in"), 16)
            sp.dma_start(wq, I["wq"]).then_inc(S("qkvw_in"), 16)
            sp.dma_start(wk, I["wk"]).then_inc(S("qkvw_in"), 16)
            sp.dma_start(wv, I["wv"]).then_inc(S("qkvw_in"), 16)
            sp.dma_start(wd0, I["w_down0"]).then_inc(S("wd0_in"), 16)
            sp.wait_ge(S("qkv_done"), 8)
            sp.dma_start(wo, I["wo"]).then_inc(S("wo_in"), 16)
            sp.dma_start(wg0, I["w_gate0"]).then_inc(S("mlp0_in"), 16)
            sp.dma_start(wu0, I["w_up0"]).then_inc(S("mlp0_in"), 16)
            sp.wait_ge(S("scatter0_done"), 4)
            sp.wait_ge(S("x1_ready"), 4)
            for dst, name in ((gw1, "gate_w1"), (wsg, "ws_gate"), (wsu, "ws_up"), (wsd, "ws_down")):
                sp.dma_start(dst, I[name]).then_inc(S("small1_in"), 16)
            sp.dma_start(bias1, I["bias1"].rearrange("(o c) -> o c", o=1).to_broadcast([P, E1])).then_inc(S("small1_in"), 16)

            def experts(g):
                if g >= 2:
                    sp.wait_ge(S("ffn1_done"), g - 1)
                r = ring[g % 2]
                e = slice(g * GE, (g + 1) * GE)
                sp.dma_start(r["g"], I["w_gate1"][:, e, :]).then_inc(S(f"ring{g % 2}_in"), 16)
                sp.dma_start(r["u"], I["w_up1"][:, e, :]).then_inc(S(f"ring{g % 2}_in"), 16)
                sp.dma_start(r["d"], I["w_down1"][:, e, :]).then_inc(S(f"ring{g % 2}_in"), 16)

            experts(0)
            experts(1)
            sp.wait_ge(S("zrow_ready"), 1)
            sp.dma_start(scratch[N:N + 1, :], zrow).then_inc(S("rows_out"), 16)
            sp.wait_ge(S("ctok1_ready"), 4)
            sp.dma_start(scratch[0:N, 0:C].rearrange("(t p) c -> p t c", p=P), ctok1).then_inc(S("rows_out"), 16)
            sp.wait_ge(S("w1_ready"), 1)
            sp.dma_start(scratch[0:N, C:ROW].rearrange("(t p) c -> p t c", p=P), w1).then_inc(S("rows_out"), 16)
            sp.wait_ge(S("v48_ready"), 1)
            sp.dma_start(slotd, v48).then_inc(S("slots_out"), 16)
            sp.wait_ge(S("slots_out"), 16)
            sp.dma_start(slotrow, slotd.rearrange("e c -> (e c)").rearrange("(t s) -> t s", s=P)).then_inc(S("slotrow_in"), 16)
            for g in range(2, NG):
                experts(g)
            sp.wait_ge(S("ffn1_done"), NG - 1)
            for dst, name in ((wup2, "w_up2"), (wga2, "w_gate2"), (aup, "up_A"), (aga, "gate_A"), (bup, "up_B"), (bga, "gate_B")):
                sp.dma_start(dst, I[name]).then_inc(S("w2a_in"), 16)
            sp.wait_ge(S("ffn1_done"), NG)
            sp.dma_start(wdn2[:, 0:5, :], I["w_down2a"]).then_inc(S("w2b_in"), 16)
            sp.dma_start(wdn2[0:64, 5, :], I["w_down2b"]).then_inc(S("w2b_in"), 16)
            sp.dma_start(adn[:, 0:5, :], I["down_Aa"]).then_inc(S("w2b_in"), 16)
            sp.dma_start(adn[0:64, 5, :], I["down_Ab"]).then_inc(S("w2b_in"), 16)
            sp.dma_start(bdn, I["down_B"]).then_inc(S("w2b_in"), 16)
            sp.wait_ge(S("x2_ready"), 4)
            sp.dma_start(gw2, I["gate_w2"]).then_inc(S("gw2_in"), 16)
            sp.wait_ge(S("ratio_ready"), LAYERS)
            sp.dma_start(wA[:], I["w3_0"]).then_inc(S("w3_in"), 16)
            sp.dma_start(wB[:], I["w3_1"]).then_inc(S("w3_in"), 16)
            sp.dma_start(wC[:], I["w3_2"]).then_inc(S("w3_in"), 16)
            for i in range(4):
                ct, ch = i % 2, i // 2
                sp.wait_ge(S("out_ready"), i + 1)
                sp.dma_start(out[:, ct, ch * CHUNK:(ch + 1) * CHUNK], r3[i % 2]).then_inc(S(f"stored{i % 2}"), 16)
            for i in range(2):
                sp.wait_ge(S(f"stored{i}"), 32)

        @block.gpsimd
        def _(pool):
            steps = [0]

            def step(ins):
                steps[0] += 1
                ins.then_inc(S("pool_step"), 1)
                pool.wait_ge(S("pool_step"), steps[0])

            g = nc.gpsimd

            def wkv_num(l):
                pool.wait_ge(S("num_scans"), l + 1)
                step(g.tensor_tensor(wA[:], wA[:], wB[:], ALU.add))
                step(g.tensor_tensor(wA[:], wA[:], ekvT[:], ALU.subtract))
                pool.wait_ge(S("euk_ready"), l + 1)
                step(g.tensor_tensor(wB[:], wD[:], kT[:], ALU.mult))
                g.tensor_tensor(wA[:], wA[:], wB[:], ALU.add).then_inc(S("num_ready"), 1)

            wkv_num(0)
            wkv_num(1)
            pool.wait_ge(S("scatter0_done"), 4)
            pool.wait_ge(S("x1_ready"), 4)
            g.memset(zrow, 0.0).then_inc(S("zrow_ready"), 1)
            for j in range(2):
                pool.wait_ge(S("shg_ready"), j + 1)
                pool.wait_ge(S("shu_read"), j + 1)
                cc = slice(j * CHUNK, (j + 1) * CHUNK)
                g.tensor_tensor(shh[:, cc], shh[:, cc], shg[:, cc], ALU.mult).then_inc(S("shh_ready"), 1)
            pool.wait_ge(S("toki_ready"), 1)
            pool.wait_ge(S("rows_out"), 48)
            for t in range(ST):
                if t >= XRING:
                    pool.wait_ge(S("xgT_done"), (t - XRING) // GT + 1)
                    pool.wait_ge(S("wslot_ready"), 1)
                g.indirect_dma_start(xg[:, t % XRING, :], None, scratch[:, :],
                                     bass.IndirectOffsetOnAxis(ap=toki[:, t:t + 1].bitcast(U32), axis=0)
                                     ).then_inc(S(f"gather{t // GT % 4}"), 16)
                if t == XRING + GT - 1:
                    wkv_num(2)
            wkv_num(3)
            pool.wait_ge(S("mb2_ready"), 4)
            g.tensor_tensor(zud, m2b, m1b, ALU.subtract).then_inc(S("mdiff_ready"), 1)
            pool.wait_ge(S("cb2_read"), 4)
            for it in range(NCH * H2T):
                ch, f = divmod(it, H2T)
                fw = H2W[f]
                su, t1, c1, t2, c2, mix = l2bufs(it)
                cc = slice(ch * CHUNK, (ch + 1) * CHUNK)
                pool.wait_ge(S("h2_ready"), 2 * it + 1)
                g.tensor_tensor(c1[0:fw], t1[0:fw], c1b[0:fw, cc], ALU.mult).then_inc(S("ch_ready"), 1)
                pool.wait_ge(S("h2_ready"), 2 * it + 2)
                g.tensor_tensor(c2[0:fw], t2[0:fw], c2b[0:fw, cc], ALU.mult).then_inc(S("ch_ready"), 1)
                pool.wait_ge(S("ch_ready"), 3 * it + 2)
                if it >= 1:
                    pool.wait_ge(S("down2_done"), it)
                g.tensor_tensor(mix[0:fw], c1[0:fw], c2[0:fw], ALU.add).then_inc(S("ch_ready"), 1)

            def round_input(ch):
                cc = slice(ch * CHUNK, (ch + 1) * CHUNK)
                m, t = mg3[:, :, cc], tmp3[:, :, cc]
                pool.wait_ge(S("mg3_ready"), ch + 1)
                step(g.tensor_tensor(t, cT[:, :, cc], m, ALU.add))
                step(g.tensor_tensor(t, t, m, ALU.subtract))
                step(g.tensor_scalar(m, t, E4_NAN, 0.0, ALU.mult, ALU.mult))
                g.tensor_tensor(c8[:, :, cc], t, m, ALU.add).then_inc(S("c8_ready"), 1)

            round_input(0)
            for it in range(NCH * F3T):
                pool.wait_ge(S("u3_ready"), it + 1)
                pool.wait_ge(S("gelu3"), it + 1)
                if it >= 2:
                    pool.wait_ge(S("a3_read"), it - 1)
                g.tensor_tensor(a3[it % 2], gg3[it % 2], u3[it % 2], ALU.mult).then_inc(S("prod3"), 1)
                if it == 1:
                    round_input(1)

        @block.scalar
        def _(act):
            steps = [0]

            def step(ins):
                steps[0] += 1
                ins.then_inc(S("act_step"), 1)
                act.wait_ge(S("act_step"), steps[0])

            s = nc.scalar

            def euk(l):
                act.wait_ge(S("euk_arg"), l + 1)
                s.activation(wD[:], wD[:], ACT.Exp).then_inc(S("euk_ready"), 1)

            def den_guess(l):
                act.wait_ge(S("den_ready"), l + 1)
                step(s.activation(ratio[l % 2][:], wC[:], ACT.Ln))
                s.activation(ratio[l % 2][:], ratio[l % 2][:], ACT.Exp, scale=-1.0).then_inc(S("guess_ready"), 1)

            def gate(l):
                for ct in range(CT):
                    if l == 0:
                        act.wait_ge(S("x_in"), 16)
                    else:
                        act.wait_ge(S(f"x{l}_ready"), 2 * ct + 2)
                    s.activation(cT[:, ct, :], xT[:, ct, :], ACT.Sigmoid).then_inc(S("sig_ready"), 1)

            def gate3(ch):
                cc = slice(ch * CHUNK, (ch + 1) * CHUNK)
                act.wait_ge(S("x3_ready"), 2 * ch + 2)
                s.activation(cT[:, :, cc], xT[:, :, cc], ACT.Sigmoid).then_inc(S("sig3_ready"), 1)

            act.wait_ge(S("vecs_in"), 16)
            step(s.activation(dw[:], vecs[:, V_W:V_W + 8], ACT.Exp))
            s.activation(dw[:], dw[:], ACT.Exp, scale=-1.0).then_inc(S("dw_ready"), 1)
            act.wait_ge(S("tsum_ready"), 1)
            s.activation(tf[:], tsum[:], ACT.Exp, scale=-1.0).then_inc(S("tfe_ready"), 1)
            act.wait_ge(S("kc_ready"), 1)
            s.activation(ekT[:], wA[:], ACT.Exp).then_inc(S("ek_ready"), 1)
            euk(0)
            gate(0)
            den_guess(0)
            for j in range(4):
                act.wait_ge(S("ctr0_done"), j + 1)
                s.copy(ctok0[:, 2 * j:2 * j + 2, :], bank[1 + j][:].rearrange("p (a c) -> p a c", a=2)).then_inc(S("ctok0_ready"), 1)
            for j in range(2):
                act.wait_ge(S("ohT_done"), j + 1)
                s.copy(onehotT[:, 4 * j:4 * j + 4, :], bank[6 + j][:].rearrange("p (a c) -> p a c", a=4)).then_inc(S("ohT_ready"), 1)
            act.wait_ge(S("ssq0"), 1)
            s.activation(col0[:, 1:2], col0[:, 1:2], ACT.Sqrt).then_inc(S("rms0"), 1)
            act.wait_ge(S("score0_ready"), 1)
            s.activation(col0[:, 8:9], col0[:, 2:3], ACT.Sigmoid).then_inc(S("gate0_ready"), 1)
            euk(1)
            for j in range(2):
                act.wait_ge(S("qkv_done"), 7 + j)
                s.copy(vtok[:, 4 * j:4 * j + 4, :], bank[6 + j][:].rearrange("p (a c) -> p a c", a=4)).then_inc(S("v_ready"), 1)
            for j in range(6):
                act.wait_ge(S("qkT_done"), j + 1)
                s.copy(qkT[:, 4 * j:4 * j + 4, :], bank[j][:].rearrange("p (a c) -> p a c", a=4)).then_inc(S("qkT_ready"), 1)
            for j in range(4):
                act.wait_ge(S("att_shifted"), j + 1)
                s.activation(att[:, 4 * j:4 * j + 4, :], att[:, 4 * j:4 * j + 4, :], ACT.Exp).then_inc(S("att_exp"), 1)
            for j in range(4):
                act.wait_ge(S("probT_done"), j + 1)
                s.copy(probT[:, 4 * j:4 * j + 4, :], bank[4 + j][:].rearrange("p (a c) -> p a c", a=4)).then_inc(S("probT_ready"), 1)
            for j in range(4):
                act.wait_ge(S("pv_done"), j + 1)
                s.copy(oT0[:, 4 * j:4 * j + 4, :], bank[j][:].rearrange("p (a c) -> p a c", a=4)).then_inc(S("oT0_ready"), 1)
            den_guess(1)
            act.wait_ge(S("ssq0"), 2)
            s.activation(col0[:, 6:7], col0[:, 6:7], ACT.Sqrt).then_inc(S("rms0"), 1)
            for j in range(2):
                act.wait_ge(S("gate0_done"), j + 1)
                s.activation(su0[:, 4 * j:4 * j + 4, :], bank[j][:].rearrange("p (a c) -> p a c", a=4), ACT.Silu).then_inc(S("silu0"), 1)
            gate(1)
            for j in range(4):
                act.wait_ge(S("ctr1_done"), j + 1)
                s.copy(ctok1[:, 2 * j:2 * j + 2, :], bank[j][:].rearrange("p (a c) -> p a c", a=2)).then_inc(S("ctok1_ready"), 1)
            act.wait_ge(S("logit1_done"), 1)
            s.activation(sc1, bank[4][:].rearrange("p (a c) -> p a c", a=NT), ACT.Sigmoid).then_inc(S("score1"), 1)
            for j in range(2):
                act.wait_ge(S("shg_done"), j + 1)
                s.activation(shg[:, j * CHUNK:(j + 1) * CHUNK], bank[5 + j][0:F1, :], ACT.Silu).then_inc(S("shg_ready"), 1)
            for j in range(2):
                act.wait_ge(S("shu_done"), j + 1)
                s.copy(shh[:, j * CHUNK:(j + 1) * CHUNK], bank[j][0:F1, :]).then_inc(S("shu_read"), 1)
            for g in range(NG):
                for ct in range(CT):
                    act.wait_ge(S("xgT_done"), g + 1)
                    if g >= 2:
                        act.wait_ge(S("gu1_done"), g - 1)
                    s.copy(xgT[g % 2][:, ct, :], bank[6 + ct][:, 0:GS]).then_inc(S("xgT_ready"), 1)
                act.wait_ge(S("gu1_done"), g + 1)
                if g >= 1:
                    act.wait_ge(S("h1_ready"), g)
                s.activation(sg1, bank[4][0:F1, 0:GS], ACT.Silu).then_inc(S("sg1_ready"), 1)
                if g in (1, 6):
                    euk(2 if g == 1 else 3)
                if g in (3, 7):
                    den_guess(2 if g == 3 else 3)
                for ct in range(CT):
                    act.wait_ge(S("ffn1_done"), g + 1)
                    if g >= 1:
                        act.wait_ge(S("outtr_done"), g)
                    s.copy(outT1[:, ct, :], bank[6 + ct][:, 0:GS]).then_inc(S("outT_ready"), 1)
            gate(2)
            for i in range(4):
                z, j = divmod(i, 2)
                act.wait_ge(S("z2_done"), i + 1)
                s.copy((zu, zg)[z][:, j * CHUNK:(j + 1) * CHUNK], bank[i][:]).then_inc(S("z2_read"), 1)
            act.wait_ge(S("shift2"), 1)
            s.activation(cw2, cw2, ACT.Exp).then_inc(S("exp2"), 1)
            for i in range(4):
                k, j = divmod(i, 2)
                act.wait_ge(S("cb2_done"), i + 1)
                s.copy((c1b, c2b)[k][:, j * CHUNK:(j + 1) * CHUNK], bank[4 + i][:]).then_inc(S("cb2_read"), 1)
            for it in range(NCH * H2T):
                fw = H2W[it % H2T]
                su, t1, c1, t2, c2, mix = l2bufs(it)
                bu = bank[2 * (it % 2)]
                for k in range(2):
                    act.wait_ge(S(("first2_done", "second2_done")[k]), it + 1)
                    if 2 * it + k >= 1:
                        act.wait_ge(S("h2_ready"), 2 * it + k)
                    s.activation(su[0:fw], bu[0:fw, :], ACT.Silu).then_inc(S("silu2"), 1)
                if it == 9:
                    gate3(0)
            gate3(1)
            for it in range(NCH * F3T):
                act.wait_ge(S("gu3_done"), it + 1)
                if it >= 2:
                    act.wait_ge(S("prod3"), it - 1)
                step(s.copy(g3[it % 2], bank[2 * (it % 2)][:]))
                s.copy(u3[it % 2], bank[2 * (it % 2) + 1][:]).then_inc(S("u3_ready"), 1)
                s.activation(gg3[it % 2], g3[it % 2], ACT.Gelu_apprx_tanh).then_inc(S("gelu3"), 1)
                if it % F3T == F3T - 1:
                    for ct in range(CT):
                        act.wait_ge(S("down3_done"), it + 1)
                        if it >= F3T:
                            act.wait_ge(S("out_ready"), ct + 1)
                        s.copy(y3[ct], bank[4 + 2 * (it // F3T) + ct][:]).then_inc(S("y3_ready"), 1)

        @block.vector
        def _(dve):
            steps = [0]

            def step(ins):
                steps[0] += 1
                ins.then_inc(S("dve_step"), 1)
                dve.wait_ge(S("dve_step"), steps[0])

            v = nc.vector

            def den_scans(l):
                for ct in range(CT):
                    for b in range(B):
                        d = dec[:, 2 * l + ct, b:b + 1].to_broadcast([P, T])
                        x = ekT[:, ct, b * T:(b + 1) * T]
                        v.tensor_tensor_scan(wC[:, ct, b * T:(b + 1) * T], d, x, 0.0, ALU.mult, ALU.add)
                        last = v.tensor_tensor_scan(back(wD, ct, b), d, back(ekT, ct, b), 0.0, ALU.mult, ALU.add)
                step(last)
                step(v.tensor_tensor(wC[:], wC[:], wD[:], ALU.add))
                for ct in range(CT):
                    last = v.tensor_scalar(wD[:, ct, :], kT[:, ct, :], vecs[:, V_U + 2 * l + ct:V_U + 2 * l + ct + 1], 30.0,
                                           ALU.add, ALU.min)
                last.then_inc(S("euk_arg"), 1)

            def back(buf, ct, b):
                return buf[:, ct, b * T:(b + 1) * T][:, ::-1]

            def num_scans(l):
                for ct in range(CT):
                    for b in range(B):
                        d = dec[:, 2 * l + ct, b:b + 1].to_broadcast([P, T])
                        v.tensor_tensor_scan(wA[:, ct, b * T:(b + 1) * T], d, ekvT[:, ct, b * T:(b + 1) * T], 0.0, ALU.mult, ALU.add)
                        last = v.tensor_tensor_scan(back(wB, ct, b), d, back(ekvT, ct, b), 0.0, ALU.mult, ALU.add)
                last.then_inc(S("num_scans"), 1)

            def den(l):
                step(v.tensor_tensor(wC[:], wC[:], ekT[:], ALU.subtract))
                dve.wait_ge(S("euk_ready"), l + 1)
                step(v.tensor_tensor(wC[:], wC[:], wD[:], ALU.add))
                v.tensor_scalar(wC[:], wC[:], 1e-8, None, ALU.max).then_inc(S("den_ready"), 1)

            def newton(l):
                y = ratio[l % 2][:]
                dve.wait_ge(S("guess_ready"), l + 1)
                step(v.tensor_tensor(wC[:], wC[:], y, ALU.mult))
                step(v.scalar_tensor_tensor(wC[:], wC[:], -2.0, y, ALU.add, ALU.mult))

            def quotient(l):
                dve.wait_ge(S("num_ready"), l + 1)
                for b in range(B):
                    last = v.scalar_tensor_tensor(ratio[l % 2][:, :, b * T:(b + 1) * T], wA[:, :, b * T:(b + 1) * T],
                                                  nosc[:, b:b + 1], wC[:, :, b * T:(b + 1) * T], ALU.mult, ALU.mult)
                last.then_inc(S("ratio_ready"), 1)
                dve.wait_ge(S("ratio_ready"), l + 1)

            def cond(l):
                for ct in range(CT):
                    dve.wait_ge(S("sig_ready"), 2 * l + ct + 1)
                    v.tensor_tensor(cT[:, ct, :], cT[:, ct, :], ratio[l % 2][:, ct, :], ALU.mult).then_inc(S("c_ready"), 1)

            dve.wait_ge(S("k_in"), 16)
            v.tensor_scalar(wA[:], kT[:], 30.0, None, ALU.min).then_inc(S("kc_ready"), 1)
            dve.wait_ge(S("cond_in"), 16)
            v.reduce_sum(tsum[:], condb[:], AX.X).then_inc(S("tsum_ready"), 1)
            dve.wait_ge(S("tfe_ready"), 1)
            step(v.tensor_scalar(tf[:], tf[:], 1.0, None, ALU.add))
            step(v.reciprocal(tf[:], tf[:]))
            step(v.tensor_scalar(dsc[:], tf[:], 0.5, 0.5, ALU.mult, ALU.add))
            step(v.tensor_scalar(nosc[:], tf[:], -0.2, -0.8, ALU.mult, ALU.add))
            dve.wait_ge(S("dw_ready"), 1)
            step(v.tensor_tensor(dec[:], dw[:].unsqueeze(2).to_broadcast([P, 8, B]),
                                 dsc[:].unsqueeze(1).to_broadcast([P, 8, B]), ALU.mult))
            dve.wait_ge(S("ek_ready"), 1)
            step(v.tensor_tensor(ekvT[:], ekT[:], kT[:], ALU.mult))
            den_scans(0)
            num_scans(0)
            step(v.memset(wbat, 0.0))
            dve.wait_ge(S("vecs_in"), 16)
            for ct in range(CT):
                last = v.tensor_copy(wbat[:, ct, ::B + 1], vecs[:, V_WR + ct:V_WR + ct + 1].to_broadcast([P, B]))
            last.then_inc(S("wbat_ready"), 1)
            den(0)
            newton(0)
            quotient(0)
            cond(0)
            dve.wait_ge(S("scores_done"), 1)
            step(v.tensor_copy(scr, bank[0][0:B, 0:T]))
            for r in range(TOP // 8):
                step(v.max(m8a, scr))
                step(v.match_replace(scr, m8a, scr, PICKED))
            dve.wait_ge(S("const_in"), 16)
            v.tensor_copy(spread4.rearrange("p (b j) -> p b j", b=B), ident[0:B, 0:B].unsqueeze(2).to_broadcast([B, B, TOP]))
            step(v.scalar_tensor_tensor(scr, scr, PICKED, desc[0:B, N - T:N], ALU.is_equal, ALU.mult))
            for r in range(TOP // 8):
                step(v.max(top4[:, 8 * r:8 * r + 8], scr))
                if r < TOP // 8 - 1:
                    step(v.match_replace(scr, top4[:, 8 * r:8 * r + 8], scr, 0.0))
            v.engine_nop().then_inc(S("top4_ready"), 1)
            dve.wait_ge(S("vb_done"), 1)
            step(v.tensor_tensor(vsel, bank[5][:, 0:TOP], jmask, ALU.mult))
            step(v.reduce_sum(col0[:, 0:1], vsel, AX.X))
            step(v.tensor_scalar(col0[:, 0:1], col0[:, 0:1], -1.0, bbase, ALU.mult, ALU.add))
            v.tensor_scalar(onehot, iota, col0[:, 0:1], None, ALU.is_equal).then_inc(S("onehot_ready"), 1)
            dve.wait_ge(S("sel_done"), 1)
            v.tensor_copy(cs, bank[5][:, 64:64 + TABW])
            step(v.tensor_copy(xs, bank[0][:, 0:C]))

            def sumsq(x, c):
                step(v.tensor_tensor(sq, x, x, ALU.mult))
                step(v.reduce_sum(col0[:, c:c + 1], sq, AX.X))
                v.tensor_scalar(col0[:, c:c + 1], col0[:, c:c + 1], 1.0 / C, 1e-6, ALU.mult, ALU.add).then_inc(S("ssq0"), 1)

            sumsq(xs, 1)
            dve.wait_ge(S("wrb_in"), 16)
            step(v.tensor_tensor(dl, xs, wrb[:], ALU.mult))
            v.reduce_sum(col0[:, 2:3], dl, AX.X).then_inc(S("score0_ready"), 1)
            dve.wait_ge(S("rms0"), 1)
            step(v.reciprocal(col0[:, 3:4], col0[:, 1:2]))
            v.tensor_scalar(xn, xs, col0[:, 3:4], None, ALU.mult).then_inc(S("xn_ready"), 1)
            dve.wait_ge(S("xnT_done"), 1)
            for ct in range(CT):
                v.tensor_scalar(hT0[:, ct, :], bank[6][:, ct * P:(ct + 1) * P], vecs[:, V_LN1 + ct:V_LN1 + ct + 1], None,
                                ALU.mult).then_inc(S("hT0_ready"), 1)
            cosb = cs[:, 0:64].unsqueeze(1).to_broadcast([P, 8, 64])
            sinb = cs[:, 64:192].unsqueeze(1).to_broadcast([P, 4, P])
            for j in range(6):
                dve.wait_ge(S("qkv_done"), j + 1)
                pj = bank[j][:].rearrange("p (h c) -> p h c", h=8)
                v.tensor_tensor(rot_a.rearrange("p (h c) -> p h c", h=8), pj, cosb, ALU.mult)
                pq = bank[j][:].rearrange("p (h a c) -> p h a c", h=4, a=2)
                for a in range(2):
                    last = v.tensor_tensor(rot_b.rearrange("p (h a c) -> p h a c", h=4, a=2)[:, :, a, :], pq[:, :, 1 - a, :],
                                           sinb[:, :, 64 * a:64 * a + 64], ALU.mult)
                step(last)
                v.tensor_tensor(qk[:, 4 * j:4 * j + 4, :], rot_a.rearrange("p (h c) -> p h c", h=4),
                                rot_b.rearrange("p (h c) -> p h c", h=4), ALU.add).then_inc(S("qk_ready"), 1)
                dve.wait_ge(S("qk_ready"), j + 1)
            den_scans(1)
            for j in range(4):
                dve.wait_ge(S("s0_done"), j + 1)
                a = att[:, 4 * j:4 * j + 4, :]
                m = mx0[:, 4 * j:4 * j + 4]
                step(v.scalar_tensor_tensor(a, bank[j][:].rearrange("p (h c) -> p h c", h=4), float(1 / np.sqrt(HD)),
                                            causal.unsqueeze(1).to_broadcast([P, 4, P]), ALU.mult, ALU.add))
                step(v.reduce_max(m, a, AX.X))
                v.tensor_tensor(a, a, m.unsqueeze(2).to_broadcast([P, 4, P]), ALU.subtract).then_inc(S("att_shifted"), 1)
            for j in range(4):
                dve.wait_ge(S("att_exp"), j + 1)
                a = att[:, 4 * j:4 * j + 4, :]
                m = sm0[:, 4 * j:4 * j + 4]
                step(v.reduce_sum(m, a, AX.X))
                step(v.reciprocal(m, m))
                v.tensor_tensor(a, a, m.unsqueeze(2).to_broadcast([P, 4, P]), ALU.mult).then_inc(S("att_ready"), 1)
            num_scans(1)
            den(1)
            dve.wait_ge(S("wo_done"), 1)
            step(v.tensor_copy(ao, bank[4][:, 0:C]))
            step(v.tensor_tensor(x1, xs, ao, ALU.add))
            sumsq(x1, 6)
            dve.wait_ge(S("rms0"), 2)
            step(v.reciprocal(col0[:, 7:8], col0[:, 6:7]))
            v.tensor_scalar(xn, x1, col0[:, 7:8], None, ALU.mult).then_inc(S("xn_ready"), 1)
            dve.wait_ge(S("xnT_done"), 2)
            for ct in range(CT):
                v.tensor_scalar(h2T0[:, ct, :], bank[6][:, ct * P:(ct + 1) * P], vecs[:, V_LN2 + ct:V_LN2 + ct + 1], None,
                                ALU.mult).then_inc(S("hT0_ready"), 1)
            newton(1)
            for j in range(2):
                dve.wait_ge(S("silu0"), j + 1)
                dve.wait_ge(S("up0_done"), j + 1)
                v.tensor_tensor(hm0[:, 4 * j:4 * j + 4, :], su0[:, 4 * j:4 * j + 4, :],
                                bank[2 + j][:].rearrange("p (a c) -> p a c", a=4), ALU.mult).then_inc(S("hm0_ready"), 1)
                if j == 0:
                    for ct in range(CT):
                        v.tensor_tensor(xT[:, ct, :], xT[:, ct, :], cT[:, ct, :], ALU.add).then_inc(S("xc0_ready"), 1)
            quotient(1)
            dve.wait_ge(S("gate0_ready"), 1)
            dve.wait_ge(S("down0_done"), 1)
            step(v.tensor_tensor(dl, bank[5][:, 0:C], ao, ALU.add))
            v.tensor_scalar(dl, dl, col0[:, 8:9], None, ALU.mult).then_inc(S("dl_ready"), 1)
            dve.wait_ge(S("xc0_ready"), CT)
            for i in range(4):
                ct, ch = divmod(i, 2)
                dve.wait_ge(S("scatter0_done"), i + 1)
                xx = xT[:, ct, ch * CHUNK:(ch + 1) * CHUNK]
                v.tensor_tensor(xx, xx, bank[i][:], ALU.add).then_inc(S("x1_ready"), 1)
            cond(1)
            dve.wait_ge(S("small1_in"), 80)
            dve.wait_ge(S("score1"), 1)
            step(v.tensor_tensor(sb1, sc1, bias1.unsqueeze(1).to_broadcast([P, NT, E1]), ALU.add))
            s8 = sb1.rearrange("p t (g e) -> p (t g) e", g=G1)
            v.tensor_tensor(hi4, s8[:, :, 0:4], s8[:, :, 4:8], ALU.max)
            step(v.tensor_tensor(lo4, s8[:, :, 0:4], s8[:, :, 4:8], ALU.min))
            v.tensor_tensor(hi2, hi4[:, :, 0:2], hi4[:, :, 2:4], ALU.max)
            v.tensor_tensor(mi2, hi4[:, :, 0:2], hi4[:, :, 2:4], ALU.min)
            step(v.tensor_tensor(lo2, lo4[:, :, 0:2], lo4[:, :, 2:4], ALU.max))
            step(v.tensor_tensor(lo2, lo2, mi2, ALU.max))
            v.tensor_tensor(hi4[:, :, 0:1], hi2[:, :, 0:1], hi2[:, :, 1:2], ALU.max)
            v.tensor_tensor(mi2[:, :, 0:1], hi2[:, :, 0:1], hi2[:, :, 1:2], ALU.min)
            step(v.tensor_tensor(lo4[:, :, 0:1], lo2[:, :, 0:1], lo2[:, :, 1:2], ALU.max))
            step(v.tensor_tensor(lo4[:, :, 0:1], lo4[:, :, 0:1], mi2[:, :, 0:1], ALU.max))
            step(v.tensor_tensor(gs1.rearrange("p t g -> p (t g)").unsqueeze(2), hi4[:, :, 0:1], lo4[:, :, 0:1], ALU.add))
            for t in range(NT):
                last = v.max(m8b[:, t, :], gs1[:, t, :])
            step(last)
            step(v.memset(m8b[:, :, KG1:8], NOWHERE))
            for t in range(NT):
                last = v.match_replace(gs1[:, t, :], m8b[:, t, :], gs1[:, t, :], PICKED)
            step(last)
            step(v.tensor_scalar(gmk, gs1.rearrange("p t g -> p (t g)"), PICKED, None, ALU.is_equal))
            v.tensor_scalar(gpn, gmk, -1.0, -LOW, ALU.add, ALU.mult)
            step(v.tensor_tensor(tm1.rearrange("p t (g e) -> p (t g) e", g=G1), s8,
                                 gmk.unsqueeze(2).to_broadcast([P, 64, 8]), ALU.mult))
            step(v.tensor_tensor(tm1.rearrange("p t (g e) -> p (t g) e", g=G1), tm1.rearrange("p t (g e) -> p (t g) e", g=G1),
                                 gpn.unsqueeze(2).to_broadcast([P, 64, 8]), ALU.add))
            for t in range(NT):
                last = v.max(m8c[:, t, :], tm1[:, t, :])
            step(last)
            step(v.memset(m8c[:, :, K1:8], NOWHERE))
            for t in range(NT):
                last = v.match_replace(tm1[:, t, :], m8c[:, t, :], tm1[:, t, :], PICKED)
            step(last)
            v.tensor_scalar(mk1, tm1, PICKED, None, ALU.is_equal).then_inc(S("mk1_ready"), 1)
            dve.wait_ge(S("mk1_ready"), 1)
            step(v.tensor_tensor(w1, mk1, sc1, ALU.mult))
            step(v.reduce_sum(ws1, w1, AX.X))
            step(v.reciprocal(wr1, ws1))
            step(v.tensor_scalar(wr1, wr1, 2.5, None, ALU.mult))
            v.tensor_tensor(w1, w1, wr1.unsqueeze(2).to_broadcast([P, NT, E1]), ALU.mult).then_inc(S("w1_ready"), 1)
            for j in range(2):
                dve.wait_ge(S("mT_done"), j + 1)
                last = v.tensor_tensor(val1[:, j * CHUNK:(j + 1) * CHUNK], bank[6 + j][0:E1, :], desc[0:E1, j * CHUNK:(j + 1) * CHUNK], ALU.mult)
            step(last)
            for r in range(CAP // 8):
                step(v.max(v48[:, 8 * r:8 * r + 8], val1))
                if r < CAP // 8 - 1:
                    step(v.match_replace(val1, v48[:, 8 * r:8 * r + 8], val1, 0.0))
            v.engine_nop().then_inc(S("v48_ready"), 1)
            dve.wait_ge(S("slotT_done"), 1)
            step(v.tensor_scalar(tokf, bank[4][:, 0:ST], -1.0, float(N), ALU.mult, ALU.add))
            v.tensor_copy(toki.bitcast(U32), tokf).then_inc(S("toki_ready"), 1)
            def slot_weights(h):
                for t in range(4):
                    dve.wait_ge(S(f"gather{t}"), 16 * GT * (h + 1))
                if h == 0:
                    dve.wait_ge(S("shdown_done"), 1)
                step(v.tensor_tensor(wsel, xg[:, :, C:ROW], emask[:, h * XRING:(h + 1) * XRING, :], ALU.mult))
                v.reduce_sum(wslot[:, h * XRING:(h + 1) * XRING], wsel, AX.X).then_inc(S("wslot_ready"), 1)
                dve.wait_ge(S("wslot_ready"), h + 1)

            slot_weights(0)
            for g in range(NG):
                if g == 4:
                    slot_weights(1)
                dve.wait_ge(S("sg1_ready"), g + 1)
                if g >= 1:
                    dve.wait_ge(S("ffn1_done"), g)
                v.tensor_tensor(h1, sg1, bank[5][0:F1, 0:GS], ALU.mult).then_inc(S("h1_ready"), 1)
                if g >= 2:
                    dve.wait_ge(S("scat1_done"), (g - 1) * GT)
                for t in range(GT):
                    i = g * GT + t
                    v.tensor_scalar(st1[g % 2][:, t, :], iota, tokf[:, i:i + 1], None, ALU.is_equal).then_inc(S("st1_ready"), 1)
                if g == 0:
                    den_scans(2)
                if g == 1:
                    num_scans(2)
                if g == 2:
                    den(2)
                if g == 4:
                    newton(2)
                    quotient(2)
                if g == 5:
                    den_scans(3)
                if g == 6:
                    num_scans(3)
                    den(3)
                dve.wait_ge(S("outtr_done"), g + 1)
                for t0, t1_, bk in ((0, 2, 4), (2, 3, 5)):
                    n = t1_ - t0
                    i = g * GT + t0
                    v.tensor_tensor(outw[:, t0:t1_, :], bank[bk][:, 0:n * C].rearrange("p (a c) -> p a c", a=n),
                                    wslot[:, i:i + n].unsqueeze(2).to_broadcast([P, n, C]), ALU.mult).then_inc(S("out1_ready"), 1)
                dve.wait_ge(S("out1_ready"), 2 * g + 2)
                for s_ in range(2):
                    step(v.tensor_copy(part1[g % 2][:, s_, :, :], outw))
                    step(v.tensor_tensor(outw, outw, part1[g % 2][:, s_, :, :], ALU.subtract))
                v.tensor_copy(part1[g % 2][:, 2, :, :], outw).then_inc(S("part1_ready"), 1)
                dve.wait_ge(S("part1_ready"), g + 1)
            newton(3)
            quotient(3)
            for i in range(4):
                ct, ch = divmod(i, 2)
                if i == 0:
                    dve.wait_ge(S("scat1_done"), ST)
                xx = xT[:, ct, ch * CHUNK:(ch + 1) * CHUNK]
                v.tensor_tensor(xx, xx, bank[i][:], ALU.add).then_inc(S("x2_ready"), 1)
            cond(2)
            dve.wait_ge(S("logit2_done"), 1)
            step(v.tensor_copy(lg2, bank[4][:, 0:NT * E2].rearrange("p (t e) -> p t e", e=E2)))
            for t in range(NT):
                last = v.max(v82[:, t, :], lg2[:, t, :])
            step(last)
            for t in range(NT):
                last = v.max_index(i82[:, t, :].bitcast(U32), v82[:, t, :], lg2[:, t, :])
            step(last)
            step(v.tensor_copy(i82f, i82.bitcast(U32)))
            v.tensor_copy(oh2[:, :, 0:2], v82[:, :, 0:2])
            for k in range(2):
                last = v.tensor_tensor(oh2[:, :, 2 + k * E2:2 + (k + 1) * E2], i82f[:, :, k:k + 1].to_broadcast([P, NT, E2]),
                                       iota[:, 0:E2].unsqueeze(1).to_broadcast([P, NT, E2]), ALU.is_equal)
            last.then_inc(S("oh2_ready"), 1)
            for j in range(2):
                dve.wait_ge(S("ohT2_done"), j + 1)
                last = v.tensor_copy(mt2[:, j * CHUNK:(j + 1) * CHUNK], bank[5 + j][0:2 + 2 * E2, :])
            for k in range(2):
                last = v.tensor_copy(spread2[:, k, :].rearrange("p (e r) -> p e r", e=E2),
                                     ident[0:2 + 2 * E2, 2 + k * E2:2 + (k + 1) * E2].unsqueeze(2).to_broadcast([2 + 2 * E2, E2, R2]))
            last.then_inc(S("mt2_ready"), 1)
            dve.wait_ge(S("mt2_ready"), 1)
            def masks(k):
                for j in range(2):
                    dve.wait_ge(S("mb2_done"), 2 * k + j + 1)
                    v.tensor_scalar((m1b, m2b)[k][:, j * CHUNK:(j + 1) * CHUNK], bank[4 + 2 * k + j][:], 2.0, None,
                                    ALU.mult).then_inc(S("mb2_ready"), 1)
                dve.wait_ge(S("mb2_ready"), 2 * k + 2)

            vt = mt2[0:2, :].rearrange("p (b t) -> p b t", b=B)
            ct2 = cw2.rearrange("p (b t) -> p b t", b=B)
            masks(0)
            dve.wait_ge(S("z2_read"), 4)
            v.tensor_tensor(zu1, zu, m1b, ALU.mult).then_inc(S("zm_ready"), 1)
            v.tensor_tensor(zg1, zg, m1b, ALU.mult).then_inc(S("zm_ready"), 1)
            masks(1)
            step(v.reduce_max(s2[:, 0:B], vt, AX.X))
            v.tensor_tensor(ct2, vt, s2[:, 0:B].unsqueeze(2).to_broadcast([2, B, T]), ALU.subtract).then_inc(S("shift2"), 1)
            dve.wait_ge(S("mdiff_ready"), 1)
            v.tensor_tensor(zgd, zg, zud, ALU.mult).then_inc(S("zm_ready"), 1)
            v.tensor_tensor(zud, zu, zud, ALU.mult).then_inc(S("zm_ready"), 1)
            dve.wait_ge(S("exp2"), 1)
            step(v.reduce_sum(s2[:, B:2 * B], ct2, AX.X))
            step(v.reciprocal(s2[:, B:2 * B], s2[:, B:2 * B]))
            v.tensor_tensor(ct2, ct2, s2[:, B:2 * B].unsqueeze(2).to_broadcast([2, B, T]), ALU.mult).then_inc(S("cw2_ready"), 1)

            def cond3(ch):
                cc = slice(ch * CHUNK, (ch + 1) * CHUNK)
                dve.wait_ge(S("sig3_ready"), ch + 1)
                step(v.tensor_tensor(cT[:, :, cc], cT[:, :, cc], ratio[3 % 2][:, :, cc], ALU.mult))
                step(v.tensor_scalar(mg3[:, :, cc].bitcast(I32), cT[:, :, cc].bitcast(I32), 0x7F800000, None, ALU.bitwise_and))
                v.tensor_scalar(mg3[:, :, cc], mg3[:, :, cc], E4_MIN, 1.5 * 2.0 ** 20, ALU.max, ALU.mult).then_inc(S("mg3_ready"), 1)

            def round_weights(i, part):
                raw, dst = ((wA, wg3[:, 0, :]), (wB, wg3[:, 1, :]), (wC, wl3))[i]
                raw, grid = raw[:].rearrange("p a b -> p (a b)"), wD[:].rearrange("p a b -> p (a b)")
                if part == 0:
                    dve.wait_ge(S("w3_in"), 48)
                    step(v.tensor_scalar(grid.bitcast(I32), raw.bitcast(I32), 0x7F800000, None, ALU.bitwise_and))
                    step(v.tensor_scalar(grid, grid, E4_MIN, 1.5 * 2.0 ** 20, ALU.max, ALU.mult))
                if part == 1:
                    step(v.tensor_tensor(raw, raw, grid, ALU.add))
                    step(v.tensor_tensor(raw, raw, grid, ALU.subtract))
                if part == 2:
                    step(v.tensor_scalar(grid, raw, E4_NAN, 0.0, ALU.mult, ALU.mult))
                    if len(dst.shape) == 3:
                        dst = dst.rearrange("p a b -> p (a b)")
                    step(v.tensor_tensor(dst, raw, grid, ALU.add))

            for it in range(NCH * H2T):
                ch, f = divmod(it, H2T)
                fw = H2W[f]
                cc = slice(ch * CHUNK, (ch + 1) * CHUNK)
                su, t1, c1, t2, c2, mix = l2bufs(it)
                bg = bank[2 * (it % 2) + 1]
                for k in range(2):
                    dve.wait_ge(S("silu2"), 2 * it + k + 1)
                    if it >= 1:
                        dve.wait_ge(S("ch_ready"), 3 * (it - 1) + k + 1)
                    v.tensor_tensor((t1, t2)[k][0:fw], su[0:fw], bg[0:fw, :], ALU.mult).then_inc(S("h2_ready"), 1)
                if it < 9:
                    round_weights(*divmod(it, 3))
                if it == 9:
                    v.engine_nop().then_inc(S("w3_ready"), 1)
                if it == 10:
                    cond3(0)
                if f == H2T - 1:
                    dve.wait_ge(S("down2_done"), it + 1)
                    d1, d2 = zu1[:, cc], zud[:, cc]
                    v.tensor_tensor(d1, bank[6][:], m1b[:, cc], ALU.mult)
                    step(v.tensor_tensor(d2, bank[7][:], m2b[:, cc], ALU.mult))
                    v.tensor_tensor(d1, d1, d2, ALU.add).then_inc(S("dm2_ready"), 1)
                    for ct in range(CT):
                        dve.wait_ge(S("y2_done"), ch + 1)
                        xx = xT[:, ct, cc]
                        v.tensor_tensor(xx, xx, bank[4 + ct][:], ALU.add).then_inc(S("x3_ready"), 1)
            cond3(1)
            for it in range(NCH * F3T):
                dve.wait_ge(S("prod3"), it + 1)
                a = a3[it % 2]
                step(v.tensor_scalar(e3.bitcast(I16), a.bitcast(I16), 0x7F80, None, ALU.bitwise_and))
                step(v.tensor_scalar(e3, e3, E4_MIN, 24.0, ALU.max, ALU.mult))
                v.tensor_tensor(b3, a, e3, ALU.add).then_inc(S("a3_read"), 1)
                dve.wait_ge(S("a3_read"), it + 1)
                step(v.tensor_tensor(b3, b3, e3, ALU.subtract))
                step(v.tensor_scalar(n3, b3, E4_NAN, 0.0, ALU.mult, ALU.mult))
                if it >= 3:
                    dve.wait_ge(S("down3_done"), it - 2)
                v.tensor_tensor(q3[it % 3], b3, n3, ALU.add).then_inc(S("q3_ready"), 1)
                if it % F3T == F3T - 1:
                    ch = it // F3T
                    for ct in range(CT):
                        dve.wait_ge(S("y3_ready"), 2 * ch + ct + 1)
                        if ch:
                            dve.wait_ge(S(f"stored{ct}"), 16)
                        v.tensor_tensor(r3[ct], xT[:, ct, ch * CHUNK:(ch + 1) * CHUNK], y3[ct], ALU.add).then_inc(S("out_ready"), 1)

        @block.tensor
        def _(pe):
            mm, tr = nc.tensor.matmul, nc.tensor.transpose

            def tokens_to_rows(banks, layer):
                for i in range(NT):
                    bk = bank[banks[i // 2]]
                    for ct in range(CT):
                        o_ = (i % 2) * C + ct * P
                        last = tr(bk[:, o_:o_ + P], cT[:, ct, i * P:(i + 1) * P], ident)
                    if i % 2:
                        last.then_inc(S(f"ctr{layer}_done"), 1)

            pe.wait_ge(S("wbat_ready"), 1)
            pe.wait_ge(S("c_ready"), 2)
            for b in range(B):
                for ct in range(CT):
                    last = mm(bank[0][0:B, 0:T], wbat[:, ct, b * B:(b + 1) * B], cT[:, ct, b * T:(b + 1) * T],
                              start=(b == 0 and ct == 0), stop=(b == B - 1 and ct == CT - 1))
            last.then_inc(S("scores_done"), 1)
            pe.wait_ge(S("const_in"), 16)
            tokens_to_rows([1, 2, 3, 4], 0)
            pe.wait_ge(S("top4_ready"), 1)
            mm(bank[5][:, 0:TOP], spread4, top4, start=True, stop=True).then_inc(S("vb_done"), 1)
            pe.wait_ge(S("onehot_ready"), 1)
            for i in range(NT):
                last = tr(bank[6 + i // 4][:, (i % 4) * P:(i % 4 + 1) * P], onehot[:, i * P:(i + 1) * P], ident)
                if i % 4 == 3:
                    last.then_inc(S("ohT_done"), 1)
            pe.wait_ge(S("ctok0_ready"), 4)
            for i in range(NT):
                pe.wait_ge(S("ohT_ready"), i // 4 + 1)
                mm(bank[0][:, 0:C], onehotT[:, i, :], ctok0[:, i, :], start=(i == 0), stop=(i == NT - 1))
            for i in range(NT):
                last = mm(bank[5][:, 64:64 + TABW], onehotT[:, i, :], table[:, i % 2, :], start=(i == 0), stop=(i == NT - 1))
            last.then_inc(S("sel_done"), 1)

            def rows_to_channels(n):
                pe.wait_ge(S("xn_ready"), n + 1)
                for ct in range(CT):
                    last = tr(bank[6][:, ct * P:(ct + 1) * P], xn[:, ct * P:(ct + 1) * P], ident)
                last.then_inc(S("xnT_done"), 1)

            rows_to_channels(0)
            pe.wait_ge(S("hT0_ready"), 2)
            pe.wait_ge(S("bias8_in"), 16)
            pe.wait_ge(S("qkvw_in"), 48)
            for j in range(8):
                w, cc = (wq, j) if j < 4 else (wk, j - 4) if j < 6 else (wv, j - 6)
                mm(bank[j][:], ident[0:8, j:j + 1].to_broadcast([8, P]), bias8, start=True, stop=False)
                for ct in range(CT):
                    last = mm(bank[j][:], hT0[:, ct, :], w[:, ct, cc * CHUNK:(cc + 1) * CHUNK], start=False, stop=(ct == CT - 1))
                last.then_inc(S("qkv_done"), 1)
            for j in range(6):
                pe.wait_ge(S("qk_ready"), j + 1)
                for i in range(4):
                    last = tr(bank[j][:, i * P:(i + 1) * P], qk[:, 4 * j + i, :], ident)
                last.then_inc(S("qkT_done"), 1)
            pe.wait_ge(S("qkT_ready"), 6)
            for j in range(4):
                for i in range(4):
                    h = 4 * j + i
                    last = mm(bank[j][:, i * P:(i + 1) * P], qkT[:, h, :], qkT[:, NH + h // 2, :], start=True, stop=True)
                last.then_inc(S("s0_done"), 1)
            pe.wait_ge(S("v_ready"), 2)
            for j in range(4):
                pe.wait_ge(S("att_ready"), j + 1)
                for i in range(4):
                    last = tr(bank[4 + j][:, i * P:(i + 1) * P], att[:, 4 * j + i, :], ident)
                last.then_inc(S("probT_done"), 1)
            for j in range(4):
                pe.wait_ge(S("probT_ready"), j + 1)
                for i in range(4):
                    h = 4 * j + i
                    last = mm(bank[j][:, i * P:(i + 1) * P], vtok[:, h // 2, :], probT[:, h, :], start=True, stop=True)
                last.then_inc(S("pv_done"), 1)
            pe.wait_ge(S("wo_in"), 16)
            for h in range(NH):
                pe.wait_ge(S("oT0_ready"), h // 4 + 1)
                last = mm(bank[4][:, 0:C], oT0[:, h, :], wo[:, h, :], start=(h == 0), stop=(h == NH - 1))
            last.then_inc(S("wo_done"), 1)
            rows_to_channels(1)
            pe.wait_ge(S("hT0_ready"), 4)
            pe.wait_ge(S("mlp0_in"), 32)
            for j in range(2):
                for w, base, name in ((wg0, 0, "gate0_done"), (wu0, 2, "up0_done")):
                    for i in range(4):
                        f = 4 * j + i
                        for ct in range(CT):
                            last = mm(bank[base + j][:, i * P:(i + 1) * P], w[:, ct, f * P:(f + 1) * P], h2T0[:, ct, :],
                                      start=(ct == 0), stop=(ct == CT - 1))
                    last.then_inc(S(name), 1)
            pe.wait_ge(S("wd0_in"), 16)
            for f in range(F0T):
                pe.wait_ge(S("hm0_ready"), f // 4 + 1)
                last = mm(bank[5][:, 0:C], hm0[:, f, :], wd0[:, f, :], start=(f == 0), stop=(f == F0T - 1))
            last.then_inc(S("down0_done"), 1)
            pe.wait_ge(S("dl_ready"), 1)
            for ct in range(CT):
                for ch in range(NCH):
                    mm(bank[2 * ct + ch][:], dl[:, ct * P:(ct + 1) * P], onehot[:, ch * CHUNK:(ch + 1) * CHUNK],
                       start=True, stop=True).then_inc(S("scatter0_done"), 1)
            pe.wait_ge(S("c_ready"), 4)
            pe.wait_ge(S("x1_ready"), 4)
            tokens_to_rows([0, 1, 2, 3], 1)
            pe.wait_ge(S("small1_in"), 80)
            for i in range(NT):
                for ct in range(CT):
                    last = mm(bank[4][:, i * E1:(i + 1) * E1], cT[:, ct, i * P:(i + 1) * P], gw1[:, ct, :],
                              start=(ct == 0), stop=(ct == CT - 1))
            last.then_inc(S("logit1_done"), 1)
            for j in range(2):
                for ct in range(CT):
                    last = mm(bank[5 + j][0:F1, :], wsg[:, ct, :], cT[:, ct, j * CHUNK:(j + 1) * CHUNK], start=(ct == 0), stop=(ct == CT - 1))
                last.then_inc(S("shg_done"), 1)
            pe.wait_ge(S("ctok1_ready"), 4)
            for j in range(2):
                for ct in range(CT):
                    last = mm(bank[j][0:F1, :], wsu[:, ct, :], cT[:, ct, j * CHUNK:(j + 1) * CHUNK], start=(ct == 0), stop=(ct == CT - 1))
                last.then_inc(S("shu_done"), 1)
            for ch in range(NCH):
                pe.wait_ge(S("shh_ready"), ch + 1)
                if ch == 0:
                    pe.wait_ge(S("shu_read"), 2)
                for ct in range(CT):
                    last = mm(bank[2 * ct + ch][:], wsd[:, ct * P:(ct + 1) * P], shh[:, ch * CHUNK:(ch + 1) * CHUNK],
                              start=True, stop=False)
            last.then_inc(S("shdown_done"), 1)
            pe.wait_ge(S("shg_ready"), 2)
            pe.wait_ge(S("mk1_ready"), 1)
            for i in range(NT):
                last = tr(bank[6 + i // 4][0:E1, (i % 4) * P:(i % 4 + 1) * P], mk1[:, i, :], ident)
                if i % 4 == 3:
                    last.then_inc(S("mT_done"), 1)
            pe.wait_ge(S("slotrow_in"), 16)
            pe.wait_ge(S("score1"), 1)
            tr(bank[4][:, 0:ST], slotrow, ident[0:ST, 0:ST]).then_inc(S("slotT_done"), 1)

            def rows_in(g):
                pe.wait_ge(S(f"gather{g % 4}"), 16 * GT * (g // 4 + 1))
                if g == 0:
                    pe.wait_ge(S("v48_ready"), 1)
                else:
                    pe.wait_ge(S("outT_ready"), 2 * g)
                for t in range(GT):
                    i = g * GT + t
                    for ct in range(CT):
                        last = tr(bank[6 + ct][:, t * P:(t + 1) * P], xg[:, i % XRING, ct * P:(ct + 1) * P], ident)
                last.then_inc(S("xgT_done"), 1)

            def gate_up(g):
                r = ring[g % 2]
                pe.wait_ge(S(f"ring{g % 2}_in"), 48 * (g // 2 + 1))
                pe.wait_ge(S("xgT_ready"), 2 * g + 2)
                if g == 0:
                    pe.wait_ge(S("toki_ready"), 1)
                    pe.wait_ge(S("shg_ready"), 2)
                else:
                    pe.wait_ge(S("out1_ready"), 2 * g)
                for bk, w in ((4, r["g"]), (5, r["u"])):
                    for e in range(GE):
                        for ct in range(CT):
                            last = mm(bank[bk][0:F1, e * CAP:(e + 1) * CAP], w[:, e, ct * F1:(ct + 1) * F1],
                                      xgT[g % 2][:, ct, e * CAP:(e + 1) * CAP], start=(ct == 0), stop=(ct == CT - 1))
                last.then_inc(S("gu1_done"), 1)

            def down(g):
                r = ring[g % 2]
                pe.wait_ge(S("h1_ready"), g + 1)
                for e in range(GE):
                    for ct in range(CT):
                        last = mm(bank[6 + ct][:, e * CAP:(e + 1) * CAP], r["d"][:, e, ct * P:(ct + 1) * P],
                                  h1[:, e * CAP:(e + 1) * CAP], start=True, stop=True)
                last.then_inc(S("ffn1_done"), 1)

            def rows_out(g):
                pe.wait_ge(S("outT_ready"), 2 * g + 2)
                for t in range(GT):
                    for ct in range(CT):
                        last = tr(bank[4 + t // 2][:, (t % 2) * C + ct * P:(t % 2) * C + (ct + 1) * P],
                                  outT1[:, ct, t * P:(t + 1) * P], ident)
                last.then_inc(S("outtr_done"), 1)

            def scatter(g, t):
                i = g * GT + t
                pe.wait_ge(S("st1_ready"), i + 1)
                pe.wait_ge(S("part1_ready"), g + 1)
                for ct in range(CT):
                    for s_ in range(3):
                        for ch in range(NCH):
                            last = mm(bank[2 * ct + ch][:], part1[g % 2][:, s_, t, ct * P:(ct + 1) * P],
                                      st1[g % 2][:, t, ch * CHUNK:(ch + 1) * CHUNK], start=False, stop=(i == ST - 1 and s_ == 2))
                last.then_inc(S("scat1_done"), 1)

            rows_in(0)
            for g in range(NG):
                gate_up(g)
                if g:
                    scatter(g - 1, 0)
                    scatter(g - 1, 1)
                down(g)
                if g:
                    scatter(g - 1, 2)
                rows_out(g)
                if g < NG - 1:
                    rows_in(g + 1)
            for t in range(GT):
                scatter(NG - 1, t)
            pe.wait_ge(S("c_ready"), 6)
            pe.wait_ge(S("gw2_in"), 16)
            for i in range(NT):
                for ct in range(CT):
                    last = mm(bank[4][:, i * E2:(i + 1) * E2], cT[:, ct, i * P:(i + 1) * P], gw2[:, ct, :],
                              start=(ct == 0), stop=(ct == CT - 1))
            last.then_inc(S("logit2_done"), 1)
            pe.wait_ge(S("x2_ready"), 4)
            pe.wait_ge(S("w2a_in"), 96)
            for i in range(4):
                z, j = divmod(i, 2)
                for ct in range(CT):
                    last = mm(bank[i][:], (aup, aga)[z][:, ct, :], cT[:, ct, j * CHUNK:(j + 1) * CHUNK],
                              start=(ct == 0), stop=(ct == CT - 1))
                last.then_inc(S("z2_done"), 1)
            pe.wait_ge(S("oh2_ready"), 1)
            W2 = 2 + 2 * E2
            for i in range(NT):
                last = tr(bank[5 + i // 4][0:W2, (i % 4) * P:(i % 4 + 1) * P], oh2[:, i, :], ident)
                if i % 4 == 3:
                    last.then_inc(S("ohT2_done"), 1)
            pe.wait_ge(S("mt2_ready"), 1)
            for i in range(4):
                k, j = divmod(i, 2)
                mm(bank[4 + i][:], spread2[:, k, :],
                   mt2[:, j * CHUNK:(j + 1) * CHUNK], start=True, stop=True).then_inc(S("mb2_done"), 1)

            def weights_to_rows():
                pe.wait_ge(S("cw2_ready"), 1)
                for i in range(4):
                    k, j = divmod(i, 2)
                    pe.wait_ge(S("mb2_ready"), i + 1)
                    mm(bank[4 + i][:], ident[0:2, k:k + 1].to_broadcast([2, P]), cw2[:, j * CHUNK:(j + 1) * CHUNK],
                       start=True, stop=True).then_inc(S("cb2_done"), 1)

            def gu2(it, k):
                ch, f = divmod(it, H2T)
                fw = H2W[f]
                cc = slice(ch * CHUNK, (ch + 1) * CHUNK)
                fs = slice(f * P, f * P + fw)
                bu, bg = bank[2 * (it % 2)], bank[2 * (it % 2) + 1]
                if k:
                    pe.wait_ge(S("h2_ready"), 2 * it + 1)
                elif it >= 2:
                    pe.wait_ge(S("h2_ready"), 2 * (it - 1))
                else:
                    pe.wait_ge(S("z2_read"), 4)
                for bk, w, lb, z in ((bu, wup2, bup, (zu1, zud)[k]), (bg, wga2, bga, (zg1, zgd)[k])):
                    if k == 0:
                        for ct in range(CT):
                            mm(bk[0:fw, :], w[:, ct, fs], cT[:, ct, cc], start=(ct == 0), stop=False, skip_group_check=True)
                    if it == 0:
                        pe.wait_ge(S("zm_ready"), 2 * k + 2)
                    last = mm(bk[0:fw, :], lb[:, fs], z[:, cc], start=False, stop=True, skip_group_check=True)
                last.then_inc(S(("first2_done", "second2_done")[k]), 1)

            def down2(it):
                ch, f = divmod(it, H2T)
                fw = H2W[f]
                su, t1, c1, t2, c2, mix = l2bufs(it)
                if it == 0:
                    pe.wait_ge(S("w2b_in"), 80)
                    pe.wait_ge(S("cb2_read"), 4)
                if f == 0 and ch:
                    pe.wait_ge(S("dm2_ready"), ch)
                    pe.wait_ge(S("x3_ready"), 2 * ch)
                pe.wait_ge(S("ch_ready"), 3 * it + 2)
                for k, cc_ in ((0, c1), (1, c2)):
                    mm(bank[6 + k][:], adn[0:fw, f, :], cc_[0:fw], start=(f == 0), stop=(f == H2T - 1))
                pe.wait_ge(S("ch_ready"), 3 * it + 3)
                for ct in range(CT):
                    last = mm(bank[4 + ct][:], wdn2[0:fw, f, ct * P:(ct + 1) * P], mix[0:fw], start=(f == 0), stop=False)
                last.then_inc(S("down2_done"), 1)

            NI = NCH * H2T
            gu2(0, 0)
            weights_to_rows()
            for it in range(NI):
                if it + 1 < NI:
                    gu2(it + 1, 0)
                gu2(it, 1)
                if it % H2T:
                    down2(it - 1)
                if it % H2T == H2T - 1:
                    ch = it // H2T
                    down2(it)
                    pe.wait_ge(S("dm2_ready"), ch + 1)
                    for ct in range(CT):
                        last = mm(bank[4 + ct][:], bdn[:, ct * P:(ct + 1) * P], zu1[:, ch * CHUNK:(ch + 1) * CHUNK],
                                  start=False, stop=True)
                    last.then_inc(S("y2_done"), 1)
            pe.wait_ge(S("w3_ready"), 1)

            def gu3(it):
                ch, f = divmod(it, F3T)
                cc = slice(ch * CHUNK, (ch + 1) * CHUNK)
                pe.wait_ge(S("c8_ready"), ch + 1)
                if it >= 2:
                    pe.wait_ge(S("u3_ready"), it - 1)
                    pe.wait_ge(S("gelu3"), it - 1)
                for bk, o_ in ((bank[2 * (it % 2)], 0), (bank[2 * (it % 2) + 1], F3)):
                    for ct in range(CT):
                        last = mm(bk[:], wg3[:, ct, o_ + f * P:o_ + (f + 1) * P], c8[:, ct, cc], start=(ct == 0), stop=(ct == CT - 1))
                last.then_inc(S("gu3_done"), 1)

            gu3(0)
            for it in range(NCH * F3T):
                ch, f = divmod(it, F3T)
                if it + 1 < NCH * F3T:
                    gu3(it + 1)
                pe.wait_ge(S("q3_ready"), it + 1)
                for ct in range(CT):
                    last = mm(bank[4 + 2 * ch + ct][:], wl3[:, f, ct * P:(ct + 1) * P], q3[it % 3], start=(f == 0), stop=(f == F3T - 1))
                last.then_inc(S("down3_done"), 1)


def constants():
    k = np.zeros((P, K_W), np.float32)
    p = np.arange(P)
    k[:, K_ID:K_ID + P] = np.eye(P)
    k[:, K_IOTA:K_IOTA + N] = np.arange(N)
    k[:, K_DESC:K_DESC + N] = N - np.arange(N)
    k[:, K_CAUS:K_CAUS + P] = np.where(p[None, :] <= p[:, None], 0.0, -1e30)
    inv = (np.float32(1.0) / np.float32(10000.0) ** (np.arange(0, HD, 2, dtype=np.float32) / np.float32(HD))).astype(np.float32)
    ang = np.arange(T, dtype=np.float32)[:, None] * inv
    tab = np.concatenate([np.cos(ang), -np.sin(ang), np.sin(ang)], axis=1)
    k[:, K_TAB:K_TAB + 2 * TABW] = tab.reshape(2, P, TABW).transpose(1, 0, 2).reshape(P, -1)
    k[:, K_JM:K_JM + TOP] = (p[:, None] % TOP == np.arange(TOP)[None, :])
    k[:, K_BB] = (p // TOP) * T + T
    slot = np.arange(SLOTS).reshape(ST, P)
    k[:, K_EM:] = (slot[:, :, None] // CAP == np.arange(E1)).transpose(1, 0, 2).reshape(P, -1)
    return k


def kernel(**inp):
    import concourse.bacc as bacc
    from concourse.bass_utils import run_bass_kernel_spmd

    a = {n: np.asarray(x) for n, x in inp.items()}

    def halves(w):
        return np.ascontiguousarray(w.reshape(-1, P, w.shape[1]).transpose(1, 0, 2))

    def cols(v):
        return v.reshape(CT, P).T

    arr = {
        "xT": halves(a["x"].reshape(N, C).T),
        "kT": halves(a["fside_BxSxS_0"].reshape(N, C).T),
        "cond": a["cond_512"],
        "vecs": np.concatenate([cols(a[f"L{l}_cond_w"]) for l in range(4)] + [cols(a[f"L{l}_cond_u"]) for l in range(4)]
                               + [cols(a["L0_ffn_w_router"]), cols(a["L0_ffn_ln1_w"]), cols(a["L0_ffn_ln2_w"])], axis=1),
        "const": constants(),
        "w_router": a["L0_ffn_w_router"],
        "qkv_b": np.concatenate([a["L0_ffn_bq"], a["L0_ffn_bk"], a["L0_ffn_bv"]]).reshape(8, CHUNK),
        "wq": halves(a["L0_ffn_wq"]), "wk": halves(a["L0_ffn_wk"]), "wv": halves(a["L0_ffn_wv"]),
        "wo": halves(a["L0_ffn_wo"]),
        "w_gate0": halves(a["L0_ffn_w_gate"]), "w_up0": halves(a["L0_ffn_w_up"]), "w_down0": halves(a["L0_ffn_w_down"]),
        "gate_w1": halves(a["L1_ffn_gate_w"]), "bias1": a["L1_ffn_bias"],
        "ws_gate": halves(a["L1_ffn_ws_gate"]), "ws_up": halves(a["L1_ffn_ws_up"]), "ws_down": a["L1_ffn_ws_down"],
        "w_gate1": a["L1_ffn_w_gate"].reshape(E1, CT, P, F1).transpose(2, 0, 1, 3).reshape(P, E1, CT * F1),
        "w_up1": a["L1_ffn_w_up"].reshape(E1, CT, P, F1).transpose(2, 0, 1, 3).reshape(P, E1, CT * F1),
        "w_down1": a["L1_ffn_w_down"].transpose(1, 0, 2),
        "gate_w2": halves(a["L2_ffn_gate_w"].T),
        "w_up2": halves(a["L2_ffn_w_up"].T), "w_gate2": halves(a["L2_ffn_w_gate"].T),
        "w_down2a": halves(a["L2_ffn_w_down"].T[0:640]), "w_down2b": a["L2_ffn_w_down"].T[640:],
        "up_A": halves(a["L2_ffn_up_A"].reshape(P, C).T), "gate_A": halves(a["L2_ffn_gate_A"].reshape(P, C).T),
        "up_B": a["L2_ffn_up_B"].transpose(0, 2, 1).reshape(P, H2),
        "gate_B": a["L2_ffn_gate_B"].transpose(0, 2, 1).reshape(P, H2),
        "down_Aa": halves(a["L2_ffn_down_A"].reshape(P, H2).T[0:640]), "down_Ab": a["L2_ffn_down_A"].reshape(P, H2).T[640:],
        "down_B": a["L2_ffn_down_B"].transpose(0, 2, 1).reshape(P, C),
    }
    w3 = a["L3_ffn_w_gating"].transpose(1, 0, 2).reshape(C, 2 * F3)
    arr["w3_0"], arr["w3_1"] = w3[0:P].reshape(P, CT, N), w3[P:].reshape(P, CT, N)
    arr["w3_2"] = halves(a["L3_ffn_w_linear"]).reshape(P, CT, N)

    nc = bacc.Bacc("TRN2", target_bir_lowering=False, num_devices=1)
    maps, aps = {}, {}
    for name, x in arr.items():
        maps["in_" + name] = np.ascontiguousarray(x)
        aps[name] = nc.dram_tensor("in_" + name, list(x.shape), mybir.dt.from_np(x.dtype), kind="ExternalInput").ap()
    out = nc.dram_tensor("out_x", [P, CT, N], F32, kind="ExternalOutput").ap()
    build(nc, aps, out)
    r = run_bass_kernel_spmd(nc, [maps], core_ids=[0])
    y = r.results[0]["out_x"]
    return np.ascontiguousarray(y.transpose(2, 1, 0).reshape(B, T, C))
```
